# Optimizing a Trainium2 kernel written in Bass

```python
import numpy as np
import jax
import jax.numpy as jnp

def _softmax(x, axis=-1):
    return jax.nn.softmax(x, axis=axis)

def _gelu(x):
    return jax.nn.gelu(x, approximate=True)

def _silu(x):
    return jax.nn.silu(x)

def _sigmoid(x):
    return jax.nn.sigmoid(x)

def _layernorm(x, axis=-1, eps=1e-05):
    m = jnp.mean(x, axis=axis, keepdims=True)
    v = jnp.var(x, axis=axis, keepdims=True)
    return (x - m) / jnp.sqrt(v + eps)

def _scatter_add(tgt, idx, src, axis=0):
    return tgt.at[idx].add(src)

def _segment_sum(src, seg, n):
    return jax.ops.segment_sum(src, seg, n)
kernel_name = 'mk_audio_tower_d1_tok_audfeat256_r4_81ca60'

def setup_inputs(seed: int=0):
    np.random.seed(seed)
    _w = jnp.asarray

    def _rec_inputs():
        import jax
        import jax.numpy as jnp
        _rk = jax.random.key(seed)
        x = 7.22013e-05 + 1.00017 * jax.random.normal(jax.random.fold_in(_rk, 1), (16, 750, 64), jnp.float32)
        return x
    x = _rec_inputs()

    def _L0_tok_setup():
        import jax, jax.numpy as jnp
        import numpy as np
        B, T, D = (8, 1024, 64)
        N_RECUR = 2
        TW = 15
        STRIDE = 2
        key = jax.random.key(seed)
        ks = jax.random.split(key, 8)
        glorot = (2.0 / (D + D)) ** 0.5
        X = jax.random.normal(ks[0], (B, T, D), dtype=jnp.float32)
        W_in = jax.random.normal(ks[1], (N_RECUR, D, D), dtype=jnp.float32) * glorot
        b_in = jax.random.normal(ks[2], (N_RECUR, D), dtype=jnp.float32) * 0.05
        W_out = jax.random.normal(ks[3], (N_RECUR, D, D), dtype=jnp.float32) * glorot
        b_out = jax.random.normal(ks[4], (N_RECUR, D), dtype=jnp.float32) * 0.05
        core_diag = jnp.ones((D,), dtype=jnp.float32)
        conv_filter = jax.random.normal(ks[5], (TW,), dtype=jnp.float32) * (2.0 / (TW + 1)) ** 0.5
        return {'X': X, 'W_in': W_in, 'b_in': b_in, 'W_out': W_out, 'b_out': b_out, 'core_diag': core_diag, 'conv_filter': conv_filter, 'stride': STRIDE}
    _L0_tok_all = _L0_tok_setup()
    _L0_tok_in = {k: v for k, v in _L0_tok_all.items() if k in ('W_in', 'b_in', 'W_out', 'b_out', 'core_diag', 'conv_filter')}
    del _L0_tok_all

    def _L0_attn_setup():
        import jax, jax.numpy as jnp
        import numpy as np
        B, S, D = (32, 512, 64)
        LN_EPS = 1e-05

        def layer_norm(x, g, b):
            mu = jnp.mean(x, axis=-1, keepdims=True)
            var = jnp.mean(jnp.square(x - mu), axis=-1, keepdims=True)
            return (x - mu) * jax.lax.rsqrt(var + LN_EPS) * g + b

        def gru_scan(x, w_ih, w_hh, b_ih, b_hh):
            H = w_hh.shape[1]
            xp = jnp.einsum('bsd,hd->bsh', x, w_ih) + b_ih
            xp = jnp.swapaxes(xp, 0, 1)
            h0 = jnp.zeros((x.shape[0], H), x.dtype)

            def step(h, xt):
                gh = h @ w_hh.T + b_hh
                r = jax.nn.sigmoid(xt[:, :H] + gh[:, :H])
                z = jax.nn.sigmoid(xt[:, H:2 * H] + gh[:, H:2 * H])
                n = jnp.tanh(xt[:, 2 * H:] + r * gh[:, 2 * H:])
                h_new = (1.0 - z) * n + z * h
                return (h_new, h_new)
            _, ys = jax.lax.scan(step, h0, xp)
            return jnp.swapaxes(ys, 0, 1)
        key = jax.random.key(seed)
        ks = jax.random.split(key, 16)
        s = 1.0 / np.sqrt(D)
        u = lambda k, shape: jax.random.uniform(k, shape, jnp.float32, -s, s)
        return {'x': jax.random.normal(ks[0], (B, S, D), jnp.float32), 'ln_g': jnp.ones((D,), jnp.float32), 'ln_b': jnp.zeros((D,), jnp.float32), 'fwd_w_ih': u(ks[1], (3 * D, D)), 'fwd_w_hh': u(ks[2], (3 * D, D)), 'fwd_b_ih': u(ks[3], (3 * D,)), 'fwd_b_hh': u(ks[4], (3 * D,)), 'rev_w_ih': u(ks[5], (3 * D, D)), 'rev_w_hh': u(ks[6], (3 * D, D)), 'rev_b_ih': u(ks[7], (3 * D,)), 'rev_b_hh': u(ks[8], (3 * D,)), 'gate_w': u(ks[9], (D, 2 * D)), 'gate_b': u(ks[10], (D,)), 'out_w': u(ks[11], (D, D)), 'out_b': u(ks[12], (D,))}
    _L0_attn_all = _L0_attn_setup()
    _L0_attn_in = {k: v for k, v in _L0_attn_all.items() if k in ('ln_g', 'ln_b', 'fwd_w_ih', 'fwd_w_hh', 'fwd_b_ih', 'fwd_b_hh', 'rev_w_ih', 'rev_w_hh', 'rev_b_ih', 'rev_b_hh', 'gate_w', 'gate_b', 'out_w', 'out_b')}
    del _L0_attn_all

    def _L0_ffn_setup():
        import jax, jax.numpy as jnp
        import numpy as np
        DIM = 64
        HEADS = 8
        NUM_KEYS = 64
        NUM_KV = NUM_KEYS ** 2
        PK_TOPK = 16
        FINAL_TOPK = 16
        DIM_KEY = DIM // 2
        P = 2

        def _pk(x, Wq_pk, pk_keys):
            b, n, _ = x.shape
            q = (x @ Wq_pk).reshape(b, n, P, HEADS, DIM_KEY).transpose(2, 0, 1, 3, 4)
            sim = jnp.einsum('pbnhd,pkhd->pbnhk', q, pk_keys)
            scores, idx = jax.lax.top_k(sim, PK_TOPK)
            idx0 = idx[0]
            idx1 = idx[1] * NUM_KEYS
            index = (idx0[..., :, None] + idx1[..., None, :]).reshape(b, n, HEADS, PK_TOPK * PK_TOPK)
            score = (scores[0][..., :, None] + scores[1][..., None, :]).reshape(b, n, HEADS, PK_TOPK * PK_TOPK)
            final_scores, pk_idx = jax.lax.top_k(score, FINAL_TOPK)
            final_indices = jnp.take_along_axis(index, pk_idx, axis=-1)
            final_scores = jax.nn.softmax(final_scores, axis=-1)
            return (final_scores, final_indices)
        key = jax.random.key(seed)
        ks = jax.random.split(key, 7)
        b, n = (2, 256)
        std = 0.02
        x = jax.random.normal(ks[0], (b, n, DIM), dtype=jnp.float32)
        Wq_pk = jax.random.normal(ks[1], (DIM, P * HEADS * DIM_KEY), dtype=jnp.float32) * std
        pk_keys = jax.random.normal(ks[2], (P, NUM_KEYS, HEADS, DIM_KEY), dtype=jnp.float32) * std
        Wq = jax.random.normal(ks[3], (DIM, HEADS * DIM), dtype=jnp.float32) * std
        keys_table = jax.random.normal(ks[4], (NUM_KV * HEADS, DIM), dtype=jnp.float32) * std
        values_table = jax.random.normal(ks[5], (NUM_KV * HEADS, DIM), dtype=jnp.float32) * std
        Wo = jax.random.normal(ks[6], (DIM * HEADS, DIM), dtype=jnp.float32) * std
        return {'x': x, 'Wq_pk': Wq_pk, 'pk_keys': pk_keys, 'Wq': Wq, 'keys_table': keys_table, 'values_table': values_table, 'Wo': Wo}
    _L0_ffn_all = _L0_ffn_setup()
    _L0_ffn_in = {k: v for k, v in _L0_ffn_all.items() if k in ('Wq_pk', 'pk_keys', 'Wq', 'keys_table', 'values_table', 'Wo')}
    del _L0_ffn_all
    return {'x': x, 'L0_tok_W_in': _L0_tok_in['W_in'], 'L0_tok_b_in': _L0_tok_in['b_in'], 'L0_tok_W_out': _L0_tok_in['W_out'], 'L0_tok_b_out': _L0_tok_in['b_out'], 'L0_tok_core_diag': _L0_tok_in['core_diag'], 'L0_tok_conv_filter': _L0_tok_in['conv_filter'], 'L0_attn_ln_g': _L0_attn_in['ln_g'], 'L0_attn_ln_b': _L0_attn_in['ln_b'], 'L0_attn_fwd_w_ih': _L0_attn_in['fwd_w_ih'], 'L0_attn_fwd_w_hh': _L0_attn_in['fwd_w_hh'], 'L0_attn_fwd_b_ih': _L0_attn_in['fwd_b_ih'], 'L0_attn_fwd_b_hh': _L0_attn_in['fwd_b_hh'], 'L0_attn_rev_w_ih': _L0_attn_in['rev_w_ih'], 'L0_attn_rev_w_hh': _L0_attn_in['rev_w_hh'], 'L0_attn_rev_b_ih': _L0_attn_in['rev_b_ih'], 'L0_attn_rev_b_hh': _L0_attn_in['rev_b_hh'], 'L0_attn_gate_w': _L0_attn_in['gate_w'], 'L0_attn_gate_b': _L0_attn_in['gate_b'], 'L0_attn_out_w': _L0_attn_in['out_w'], 'L0_attn_out_b': _L0_attn_in['out_b'], 'L0_ffn_Wq_pk': _L0_ffn_in['Wq_pk'], 'L0_ffn_pk_keys': _L0_ffn_in['pk_keys'], 'L0_ffn_Wq': _L0_ffn_in['Wq'], 'L0_ffn_keys_table': _L0_ffn_in['keys_table'], 'L0_ffn_values_table': _L0_ffn_in['values_table'], 'L0_ffn_Wo': _L0_ffn_in['Wo']}

def reference(x, L0_tok_W_in, L0_tok_b_in, L0_tok_W_out, L0_tok_b_out, L0_tok_core_diag, L0_tok_conv_filter, L0_attn_ln_g, L0_attn_ln_b, L0_attn_fwd_w_ih, L0_attn_fwd_w_hh, L0_attn_fwd_b_ih, L0_attn_fwd_b_hh, L0_attn_rev_w_ih, L0_attn_rev_w_hh, L0_attn_rev_b_ih, L0_attn_rev_b_hh, L0_attn_gate_w, L0_attn_gate_b, L0_attn_out_w, L0_attn_out_b, L0_ffn_Wq_pk, L0_ffn_pk_keys, L0_ffn_Wq, L0_ffn_keys_table, L0_ffn_values_table, L0_ffn_Wo):
    import jax
    import jax.numpy as jnp

    def _L0_tok_ref(X, W_in, b_in, W_out, b_out, core_diag, conv_filter, stride):
        import jax, jax.numpy as jnp
        import numpy as np
        B, T, D = (8, 1024, 64)
        N_RECUR = 2
        TW = 15
        STRIDE = 2
        out = X
        for i in range(W_in.shape[0]):
            out = jnp.tanh(out @ W_in[i] + b_in[i])
        out = jnp.abs(core_diag)[None, None, :] * out * out
        n = W_out.shape[0]
        for i in range(n):
            out = jnp.tanh(out @ W_out[n - 1 - i] + b_out[n - 1 - i])
        tw = conv_filter.shape[0]
        pad = tw // 2
        out = jnp.pad(out, ((0, 0), (pad, pad), (0, 0)))
        d = out.shape[-1]
        kernel = jnp.broadcast_to(conv_filter[:, None, None], (tw, 1, d))
        out_pool = jax.lax.conv_general_dilated(out, kernel, window_strides=(stride,), padding='VALID', dimension_numbers=('NWC', 'WIO', 'NWC'), feature_group_count=d)
        return out_pool

    def _L0_attn_ref(x, ln_g, ln_b, fwd_w_ih, fwd_w_hh, fwd_b_ih, fwd_b_hh, rev_w_ih, rev_w_hh, rev_b_ih, rev_b_hh, gate_w, gate_b, out_w, out_b):
        import jax, jax.numpy as jnp
        import numpy as np
        B, S, D = (32, 512, 64)
        LN_EPS = 1e-05

        def layer_norm(x, g, b):
            mu = jnp.mean(x, axis=-1, keepdims=True)
            var = jnp.mean(jnp.square(x - mu), axis=-1, keepdims=True)
            return (x - mu) * jax.lax.rsqrt(var + LN_EPS) * g + b

        def gru_scan(x, w_ih, w_hh, b_ih, b_hh):
            H = w_hh.shape[1]
            xp = jnp.einsum('bsd,hd->bsh', x, w_ih) + b_ih
            xp = jnp.swapaxes(xp, 0, 1)
            h0 = jnp.zeros((x.shape[0], H), x.dtype)

            def step(h, xt):
                gh = h @ w_hh.T + b_hh
                r = jax.nn.sigmoid(xt[:, :H] + gh[:, :H])
                z = jax.nn.sigmoid(xt[:, H:2 * H] + gh[:, H:2 * H])
                n = jnp.tanh(xt[:, 2 * H:] + r * gh[:, 2 * H:])
                h_new = (1.0 - z) * n + z * h
                return (h_new, h_new)
            _, ys = jax.lax.scan(step, h0, xp)
            return jnp.swapaxes(ys, 0, 1)
        residual = x
        xn = layer_norm(x, ln_g, ln_b)
        fwd_out = gru_scan(xn, fwd_w_ih, fwd_w_hh, fwd_b_ih, fwd_b_hh)
        rev_out = gru_scan(xn[:, ::-1], rev_w_ih, rev_w_hh, rev_b_ih, rev_b_hh)[:, ::-1]
        g = jax.nn.sigmoid(jnp.concatenate([fwd_out, rev_out], axis=-1) @ gate_w.T + gate_b)
        combined = g * fwd_out + (1.0 - g) * rev_out
        out = combined @ out_w.T + out_b
        return out + residual

    def _L0_ffn_ref(x, Wq_pk, pk_keys, Wq, keys_table, values_table, Wo):
        import jax, jax.numpy as jnp
        import numpy as np
        DIM = 64
        HEADS = 8
        NUM_KEYS = 64
        NUM_KV = NUM_KEYS ** 2
        PK_TOPK = 16
        FINAL_TOPK = 16
        DIM_KEY = DIM // 2
        P = 2

        def _pk(x, Wq_pk, pk_keys):
            b, n, _ = x.shape
            q = (x @ Wq_pk).reshape(b, n, P, HEADS, DIM_KEY).transpose(2, 0, 1, 3, 4)
            sim = jnp.einsum('pbnhd,pkhd->pbnhk', q, pk_keys)
            scores, idx = jax.lax.top_k(sim, PK_TOPK)
            idx0 = idx[0]
            idx1 = idx[1] * NUM_KEYS
            index = (idx0[..., :, None] + idx1[..., None, :]).reshape(b, n, HEADS, PK_TOPK * PK_TOPK)
            score = (scores[0][..., :, None] + scores[1][..., None, :]).reshape(b, n, HEADS, PK_TOPK * PK_TOPK)
            final_scores, pk_idx = jax.lax.top_k(score, FINAL_TOPK)
            final_indices = jnp.take_along_axis(index, pk_idx, axis=-1)
            final_scores = jax.nn.softmax(final_scores, axis=-1)
            return (final_scores, final_indices)
        b, n, d = x.shape
        q = (x @ Wq).reshape(b, n, HEADS, DIM) * DIM ** (-0.5)
        kv_scores, indices = _pk(x, Wq_pk, pk_keys)
        offsets = jnp.arange(HEADS, dtype=indices.dtype) * NUM_KV
        ind = indices + offsets[None, None, :, None]
        k = jnp.einsum('bnhk,bnhkd->bnhd', kv_scores, keys_table[ind])
        v = jnp.einsum('bnhk,bnhkd->bnhd', kv_scores, values_table[ind])
        sim = jnp.einsum('bihd,bjhd->bhij', q, k)
        neg = -jnp.finfo(sim.dtype).max
        causal = jnp.tril(jnp.ones((n, n), dtype=bool))
        sim = jnp.where(causal, sim, neg)
        attn = jax.nn.softmax(sim, axis=-1)
        out = jnp.einsum('bhij,bjhd->bhid', attn, v)
        out = out.transpose(0, 2, 1, 3).reshape(b, n, HEADS * DIM)
        return out @ Wo
    h = _L0_tok_ref(x, L0_tok_W_in, L0_tok_b_in, L0_tok_W_out, L0_tok_b_out, L0_tok_core_diag, L0_tok_conv_filter, 2)
    h = h + _L0_attn_ref(_layernorm(h, axis=-1), L0_attn_ln_g, L0_attn_ln_b, L0_attn_fwd_w_ih, L0_attn_fwd_w_hh, L0_attn_fwd_b_ih, L0_attn_fwd_b_hh, L0_attn_rev_w_ih, L0_attn_rev_w_hh, L0_attn_rev_b_ih, L0_attn_rev_b_hh, L0_attn_gate_w, L0_attn_gate_b, L0_attn_out_w, L0_attn_out_b)
    h = h + _L0_ffn_ref(_layernorm(h, axis=-1), L0_ffn_Wq_pk, L0_ffn_pk_keys, L0_ffn_Wq, L0_ffn_keys_table, L0_ffn_values_table, L0_ffn_Wo)
    return h

_drawn_inputs = setup_inputs


def setup_inputs(seed=0):
    import zlib

    import numpy as np

    out = dict(_drawn_inputs(seed))
    spreads = {'L0_tok_core_diag': (1.0, 0.2), 'L0_attn_ln_g': (1.0, 0.6), 'L0_attn_ln_b': (0.0, 0.558)}
    factors = {'L0_attn_fwd_w_hh': 2.907,
     'L0_attn_fwd_b_ih': 5.897,
     'L0_attn_fwd_b_hh': 8.0,
     'L0_attn_rev_w_hh': 3.361,
     'L0_attn_rev_b_ih': 4.79,
     'L0_attn_rev_b_hh': 8.0,
     'L0_attn_gate_b': 8.0,
     'L0_ffn_Wq_pk': 8.0,
     'L0_ffn_pk_keys': 8.0,
     'L0_ffn_Wq': 64.0,
     'L0_ffn_keys_table': 64.0,
     'L0_ffn_values_table': 8.0,
     'L0_ffn_Wo': 8.0}
    for name, (base, spread) in spreads.items():
        noise = np.random.default_rng([zlib.crc32(name.encode()), seed]).standard_normal(out[name].shape)
        drawn = base * np.exp(spread * noise) if base else spread * noise
        out[name] = jnp.asarray(drawn.astype(out[name].dtype))
    for name, factor in factors.items():
        out[name] = (out[name] * factor).astype(out[name].dtype)
    return out
```

```python
from contextlib import ExitStack

import numpy as np

import concourse.bass as bass
from concourse import mybir

ALU = mybir.AluOpType
ACT = mybir.ActivationFunctionType
AX_X = mybir.AxisListType.X
F32 = mybir.dt.float32
U32 = mybir.dt.uint32

B, T_IN, D = 16, 750, 64
TAPS, STRIDE = 15, 2
T = (T_IN - 1) // STRIDE + 1
PAD = TAPS // 2
PAIRS = B // 2
H, K, NK = 8, 16, 64
TT = 125
NT = T // TT
BLK = T_IN // TT
EPS = 1e-5
LOWEST = -3.0e38
HK = H * K
SEGMENTS = []
for _a in range(K):
    _nb = K // (_a + 1)
    if SEGMENTS and SEGMENTS[-1][2] == _nb:
        SEGMENTS[-1][1] += 1
    else:
        SEGMENTS.append([_a, 1, _nb])
CAND = sum(na * nb for _, na, nb in SEGMENTS)
GROUP = 5
NG = TT // GROUP

FIELDS = [
    ("ident", 128), ("mean", 128), ("vecs", 4 + 3 + TAPS + 6 + 3), ("gatew", 64), ("diff", 64),
    ("pickrev", 64), ("outw", 64), ("mask8", H), ("iota", CAND), ("causal", T + TT),
    ("headoff", H), ("wq", 512), ("wo", 512),
]
EARLY = [
    ("win0", 128), ("win1", 128), ("wout1", 128), ("wout0", 128), ("wih", 384), ("whh", 384),
    ("wqpkT", 256), ("keys", 1024),
]
WIDTH = sum(w for _, w in FIELDS)
EARLY_WIDTH = sum(w for _, w in EARLY)
V_BTOK, V_CORE, V_LNG, V_LNB, V_FILT = 0, 4, 5, 6, 7
V_BIH = V_FILT + TAPS
V_BHH = V_BIH + 3
V_GATEB = V_BHH + 3
V_OUTB = V_GATEB + 1
V_EPS = V_OUTB + 1


def fields(tensor, names):
    views, at = {}, 0
    for name, width in names:
        views[name] = tensor[:, at:at + width]
        at += width
    return views


def build(nc, x, pack, early, table, out):
    resid = nc.dram_tensor("resid", (B, D, T), F32).ap()
    with ExitStack() as ctx:
        cst = ctx.enter_context(nc.sbuf_tensor("cst", [128, WIDTH], F32))
        hist = ctx.enter_context(nc.sbuf_tensor("hist", [128, T, B], F32))
        keymat = ctx.enter_context(nc.sbuf_tensor("keymat", [64, 1024], F32))
        ps = ctx.enter_context(nc.psum_tensor("ps", [128, 8, 512], F32))
        col = fields(cst, FIELDS)
        with ExitStack() as until_gru:
            def sb(name, shape):
                return until_gru.enter_context(nc.sbuf_tensor(name, shape, F32))
            first = sb("early", [128, EARLY_WIDTH])
            derived = sb("derived", [128, 8])
            steps = sb("steps", [128, T, B])
            both = {**col, **fields(first, EARLY)}
            token_mixer(nc, x, (pack, early), (cst, first), both, derived, steps, resid, ps)
            states = sb("states", [128, T, B])
            gru(nc, both, derived, steps, states, ps)
            turn_and_fold(nc, both, states, hist, keymat, ps)
        attention(nc, col, keymat, table, out, resid, hist, ps)


def token_mixer(nc, x, packs, csts, col, derived, steps, resid, ps):
    vec = col["vecs"]
    with ExitStack() as ctx:
        def sb(name, shape):
            return ctx.enter_context(nc.sbuf_tensor(name, shape, F32))

        def sem(name):
            return ctx.enter_context(nc.semaphore(name))

        xin = [sb(f"xin{u}", [TT, BLK, 2, 64]) for u in range(2)]
        xT = [sb(f"xT{u}", [128, T_IN]) for u in range(2)]
        one = [sb(f"layer_a{u}", [128, T_IN]) for u in range(2)]
        two = [sb(f"layer_b{u}", [128, T_IN]) for u in range(2)]
        padded = [sb(f"padded{u}", [128, T_IN + 2 * PAD]) for u in range(2)]
        hT = [sb(f"hT{u}", [128, T]) for u in range(2)]
        cen = [sb(f"cen{u}", [128, T]) for u in range(2)]
        sq = [sb(f"sq{u}", [128, T]) for u in range(2)]
        sd = [sb(f"sd{u}", [128, T]) for u in range(2)]
        nrm = [sb(f"nrm{u}", [128, T]) for u in range(2)]
        res = [sb(f"res{u}", [128, T]) for u in range(2)]
        xn = [sb(f"xn{u}", [128, T]) for u in range(2)]

        s_cst = sem("a_consts_loaded")
        s_x = [sem(f"a_x_loaded{u}") for u in range(2)]
        s_pad = sem("a_pads_zeroed")
        s_tr = sem("a_x_transposed")
        s_xT = sem("a_xT_copied")
        s_mm = sem("a_layer_product")
        s_th = sem("a_tanh_done")
        s_sq = sem("a_squared_by_core")
        s_stat = sem("a_statistic_product")
        s_dve = sem("a_vector_chain")
        s_cen = sem("a_centred")
        s_csq = sem("a_centred_squared")
        s_sd = sem("a_deviation")
        s_rec = sem("a_deviation_inverted")
        s_nrm = sem("a_normed")
        s_xn = sem("a_gru_input_ready")
        s_put = sem("a_gru_input_placed")
        s_put2 = sem("a_gru_input_placed_pool")
        s_res = [sem(f"a_resid_stored{u}") for u in range(2)]
        s_free = sem("a_resid_buffer_free")
        s_setup = sem("a_setup_done")

        block = ctx.enter_context(nc.Block())

        @block.sync
        def _(sp):
            for dst, src in zip(csts, packs):
                sp.dma_start(dst[:], src[:]).then_inc(s_cst, 16)
            with sp.Fori(0, PAIRS // 2) as g:
                for u in range(2):
                    sp.wait_ge(s_tr, g * 2 + (u + 1))
                    for half in range(2):
                        src = x[bass.ds(g * 2 + (u + 8 * half), 1)].rearrange("o (p k) d -> p (o k) d", k=BLK)
                        sp.dma_start(xin[u][:, :, half, :], src).then_inc(s_x[u], 16)

        @block.tensor
        def _(pe):
            pe.wait_ge(s_cst, 32)
            nc.tensor.nop().then_inc(s_tr, 2)
            banks = [ps[:, 4 * u:4 * u + 4, :] for u in range(2)]

            def layer(g, u, k, weight, src):
                for j in range(2):
                    mm = nc.tensor.matmul(banks[u][:, 2 + j, 0:T], weight, src[:, j * T:(j + 1) * T],
                                          start=True, stop=True)
                mm.then_inc(s_mm, 1)

            def stat(u, bank, src):
                nc.tensor.matmul(banks[u][:, bank, 0:T], col["mean"], src[:, :],
                                 start=True, stop=True).then_inc(s_stat, 1)

            with pe.Fori(0, PAIRS // 2) as g:
                for u in range(2):
                    pe.wait_ge(s_x[u], g * 32 + 32)
                    pe.wait_ge(s_xn, g * 2 + (u + 1))
                    for k in range(BLK):
                        tr = nc.tensor.transpose(banks[u][:, k // 3, (k % 3) * TT:(k % 3 + 1) * TT],
                                                 xin[u][:, k].rearrange("p a d -> p (a d)"), col["ident"][0:TT, 0:TT])
                    tr.then_inc(s_tr, 1)
                for u in range(2):
                    pe.wait_ge(s_xT, g * 2 + (u + 1))
                    layer(g, u, 0, col["win0"], xT[u])
                for u in range(2):
                    pe.wait_ge(s_th, g * 8 + (u + 1))
                    layer(g, u, 1, col["win1"], one[u])
                for u in range(2):
                    pe.wait_ge(s_sq, g * 2 + (u + 1))
                    layer(g, u, 2, col["wout1"], one[u])
                for u in range(2):
                    pe.wait_ge(s_th, g * 8 + (4 + u + 1))
                    layer(g, u, 3, col["wout0"], two[u])
                for u in range(2):
                    pe.wait_ge(s_nrm, g * 6 + (u + 1))
                    stat(u, 0, hT[u])
                for u in range(2):
                    pe.wait_ge(s_csq, g * 4 + (u + 1))
                    stat(u, 1, sq[u])
                for u in range(2):
                    pe.wait_ge(s_nrm, g * 6 + (2 + u + 1))
                    stat(u, 0, nrm[u])
                for u in range(2):
                    pe.wait_ge(s_csq, g * 4 + (2 + u + 1))
                    stat(u, 1, sq[u])

        @block.scalar
        def _(act):
            act.wait_ge(s_cst, 32)
            nc.scalar.activation(derived[:, 4:5], vec[:, V_CORE:V_CORE + 1], ACT.Abs).then_inc(s_setup, 1)
            act.wait_ge(s_pad, 4)
            with act.Fori(0, PAIRS // 2) as g:
                def tanh(g, u, k, dst):
                    act.wait_ge(s_mm, g * 8 + (2 * k + u + 1))
                    src = ps[:, 4 * u + 2:4 * u + 4, 0:T]
                    nc.scalar.activation(dst.rearrange("p (a b) -> p a b", a=2), src, ACT.Tanh,
                                         bias=vec[:, V_BTOK + k:V_BTOK + k + 1]).then_inc(s_th, 1)
                for u in range(2):
                    tanh(g, u, 0, one[u][:, :])
                for u in range(2):
                    tanh(g, u, 1, two[u][:, :])
                for u in range(2):
                    tanh(g, u, 2, two[u][:, :])
                for u in range(2):
                    act.wait_ge(s_cen, g * 4 + (u + 1))
                    tanh(g, u, 3, padded[u][:, PAD:PAD + T_IN])
                for v in range(2):
                    for u in range(2):
                        act.wait_ge(s_cen, g * 4 + (2 + 2 * v + u + 1))
                        nc.scalar.activation(sq[u][:, :], cen[u][:, :], ACT.Square).then_inc(s_csq, 1)
                    for u in range(2):
                        act.wait_ge(s_stat, g * 8 + (4 * v + 2 + u + 1))
                        nc.scalar.activation(sd[u][:, :], ps[:, 4 * u + 1, 0:T], ACT.Sqrt,
                                             bias=vec[:, V_EPS:V_EPS + 1]).then_inc(s_sd, 1)
                for u in range(2):
                    act.wait_ge(s_xn, g * 2 + (2 + u + 1))
                    nc.scalar.copy(steps[0:64, :, bass.ds(g * 2 + u, 1)], xn[u][0:64, :].unsqueeze(2))
                    nc.scalar.copy(steps[64:128, :, bass.ds(g * 2 + u, 1)], xn[u][0:64, ::-1].unsqueeze(2))
                    nc.scalar.copy(steps[0:64, :, bass.ds(g * 2 + (u + 8), 1)], xn[u][64:128, :].unsqueeze(2)).then_inc(s_put, 1)

        @block.gpsimd
        def _(pool):
            for u in range(2):
                nc.gpsimd.memset(padded[u][:, 0:PAD], 0.0).then_inc(s_pad, 1)
                nc.gpsimd.memset(padded[u][:, PAD + T_IN:], 0.0).then_inc(s_pad, 1)
            with pool.Fori(0, PAIRS // 2) as g:
                for u in range(2):
                    pool.wait_ge(s_xn, g * 2 + (2 + u + 1))
                    nc.gpsimd.tensor_copy(steps[64:128, :, bass.ds(g * 2 + (u + 8), 1)], xn[u][64:128, ::-1].unsqueeze(2)).then_inc(s_put2, 1)
                    for half in range(2):
                        pool.dma_start(resid[bass.ds(g * 2 + (u + 8 * half), 1)].rearrange("o d t -> (o d) t"),
                                       res[u][64 * half:64 * half + 64, :]).then_inc(s_res[u], 16)
                for u in range(2):
                    pool.wait_ge(s_res[u], g * 32 + 32)
                    pool.sem_inc(s_free, 1)

        @block.vector
        def _(dve):
            dve.wait_ge(s_cst, 32)
            nc.vector.tensor_tensor(derived[:, 0:3], vec[:, V_BIH:V_BIH + 3], vec[:, V_BHH:V_BHH + 3], ALU.add).then_inc(s_setup, 1)
            dve.wait_ge(s_setup, 2)
            nc.vector.tensor_scalar(derived[:, 3:4], derived[:, 1:2], -1.0, None, ALU.mult).then_inc(s_xn, 2)
            nc.vector.nop().then_inc(s_cen, 2)
            nc.vector.nop().then_inc(s_put, 2)
            nc.vector.nop().then_inc(s_put2, 2)
            nc.vector.nop().then_inc(s_free, 2)
            dve.wait_ge(s_pad, 4)
            with dve.Fori(0, PAIRS // 2) as g:
                for u in range(2):
                    dve.wait_ge(s_tr, g * 2 + (2 + u + 1))
                    for half in range(2):
                        cp = nc.vector.tensor_copy(
                            xT[u][:, :].rearrange("f (p k) -> f k p", k=BLK)[:, 3 * half:3 * half + 3],
                            ps[:, 4 * u + half, 0:T].rearrange("f (k p) -> f k p", k=3))
                    cp.then_inc(s_xT, 1)
                for u in range(2):
                    dve.wait_ge(s_th, g * 8 + (2 + u + 1))
                    nc.vector.scalar_tensor_tensor(one[u][:, :], two[u][:, :], derived[:, 4:5], two[u][:, :],
                                                   ALU.mult, ALU.mult).then_inc(s_sq, 1)
                for k in range(TAPS):
                    for u in range(2):
                        taps = padded[u][:, k:k + 2 * T - 1:STRIDE]
                        f = vec[:, V_FILT + k:V_FILT + k + 1]
                        done = s_nrm if k == TAPS - 1 else s_dve
                        if k == 0:
                            dve.wait_ge(s_th, g * 8 + (6 + u + 1))
                            nc.vector.tensor_scalar(hT[u][:, :], taps, f, None, ALU.mult).then_inc(done, 1)
                        else:
                            dve.wait_ge(s_dve, g * (2 * TAPS) + (2 * (k - 1) + u + 1))
                            nc.vector.scalar_tensor_tensor(hT[u][:, :], taps, f, hT[u][:, :],
                                                           ALU.mult, ALU.add).then_inc(done, 1)
                for v in range(2):
                    for u in range(2):
                        dve.wait_ge(s_stat, g * 8 + (4 * v + u + 1))
                        src = (hT, nrm)[v][u]
                        nc.vector.tensor_tensor(cen[u][:, :], src[:, :], ps[:, 4 * u, 0:T],
                                                ALU.subtract).then_inc(s_cen, 1)
                    for u in range(2):
                        dve.wait_ge(s_sd, g * 4 + (2 * v + u + 1))
                        nc.vector.reciprocal(sd[u][:, :], sd[u][:, :]).then_inc(s_rec, 1)
                    for u in range(2):
                        dve.wait_ge(s_cen, g * 4 + (2 + 2 * v + u + 1))
                        dve.wait_ge(s_rec, g * 4 + (2 * v + u + 1))
                        if v == 1:
                            dve.wait_ge(s_put, g * 2 + (u + 1))
                            dve.wait_ge(s_put2, g * 2 + (u + 1))
                        nc.vector.tensor_tensor((nrm, xn)[v][u][:, :], cen[u][:, :], sd[u][:, :],
                                                ALU.mult).then_inc(s_nrm, 1)
                    if v == 0:
                        for u in range(2):
                            dve.wait_ge(s_nrm, g * 6 + (2 + u + 1))
                            dve.wait_ge(s_free, g * 2 + (u + 1))
                            nc.vector.tensor_tensor(res[u][:, :], hT[u][:, :], nrm[u][:, :], ALU.add).then_inc(s_dve, 1)
                for u in range(2):
                    dve.wait_ge(s_nrm, g * 6 + (4 + u + 1))
                    dve.wait_ge(s_dve, g * (2 * TAPS) + (2 * TAPS - 2 + u + 1))
                    nc.vector.tensor_scalar(xn[u][:, :], xn[u][:, :], vec[:, V_LNG:V_LNG + 1], vec[:, V_LNB:V_LNB + 1],
                                            ALU.mult, ALU.add).then_inc(s_xn, 1)


UNROLL = 22


def gru(nc, col, derived, steps, hist, ps):
    vec = col["vecs"]
    with ExitStack() as ctx:
        def sb(name, shape):
            return ctx.enter_context(nc.sbuf_tensor(name, shape, F32))

        def sem(name):
            return ctx.enter_context(nc.semaphore(name))

        r = sb("r", [128, 2, B])
        z = sb("z", [128, 2, B])
        omz = sb("one_minus_z", [128, 2, B])
        rn = sb("r_times_n", [128, 2, B])
        pre = sb("n_before_tanh", [128, 2, B])
        n = sb("n", [128, 2, B])
        m = sb("m", [128, 2, B])
        zh = sb("zh", [128, 2, B])
        s_r, s_n, s_z = sem("g_r_product"), sem("g_n_product"), sem("g_z_product")
        s_rs, s_zs, s_ns = sem("g_r_sigmoid"), sem("g_z_sigmoid"), sem("g_n_tanh")
        s_rn, s_pre = sem("g_r_times_n"), sem("g_n_before_tanh")
        s_omz, s_zh, s_m, s_h = sem("g_one_minus_z"), sem("g_zh"), sem("g_m"), sem("g_h")

        wih = [col["wih"][:, g * 128:(g + 1) * 128] for g in range(3)]
        whh = [col["whh"][:, g * 128:(g + 1) * 128] for g in range(3)]
        block = ctx.enter_context(nc.Block())
        rounds = (T - 1) // UNROLL
        assert rounds * UNROLL == T - 1 and UNROLL % 2 == 0

        def run(eng, step):
            step(0, 0, True)
            with eng.Fori(0, rounds) as i:
                for j in range(UNROLL):
                    step(i * UNROLL + (j + 1), (j + 1) % 2, False)

        @block.tensor
        def _(pe):
            def step(s, k, first):
                xs = steps[:, bass.ds(s, 1), :].rearrange("p o b -> p (o b)")
                bank = [ps[:, 4 * k + q, 0:B] for q in range(4)]
                if first:
                    nc.tensor.matmul(bank[0], wih[0], xs, start=True, stop=True).then_inc(s_r, 1)
                    nc.tensor.matmul(bank[3], wih[2], xs, start=True, stop=True).then_inc(s_n, 1)
                    nc.tensor.matmul(bank[1], wih[1], xs, start=True, stop=True).then_inc(s_z, 1)
                    return
                nc.tensor.matmul(bank[0], wih[0], xs, start=True, stop=False)
                nc.tensor.matmul(bank[3], wih[2], xs, start=True, stop=True)
                nc.tensor.matmul(bank[1], wih[1], xs, start=True, stop=False)
                pe.wait_ge(s_zh, s)
                nc.tensor.matmul(bank[0], whh[0], zh[:, 1 - k, :], start=False, stop=False)
                nc.tensor.matmul(bank[2], whh[2], zh[:, 1 - k, :], start=True, stop=False)
                nc.tensor.matmul(bank[1], whh[1], zh[:, 1 - k, :], start=False, stop=False)
                pe.wait_ge(s_m, s)
                nc.tensor.matmul(bank[0], whh[0], m[:, 1 - k, :], start=False, stop=True).then_inc(s_r, 1)
                nc.tensor.matmul(bank[2], whh[2], m[:, 1 - k, :], start=False, stop=True).then_inc(s_n, 1)
                nc.tensor.matmul(bank[1], whh[1], m[:, 1 - k, :], start=False, stop=True).then_inc(s_z, 1)
            run(pe, step)

        @block.scalar
        def _(act):
            def step(s, k, first):
                act.wait_ge(s_r, s + 1)
                nc.scalar.activation(r[:, k, :], ps[:, 4 * k, 0:B], ACT.Sigmoid, bias=derived[:, 0:1]).then_inc(s_rs, 1)
                act.wait_ge(s_z, s + 1)
                nc.scalar.activation(z[:, k, :], ps[:, 4 * k + 1, 0:B], ACT.Sigmoid, bias=derived[:, 1:2]).then_inc(s_zs, 1)
                act.wait_ge(s_pre, s + 1)
                nc.scalar.activation(n[:, k, :], pre[:, k, :], ACT.Tanh, bias=vec[:, V_BIH + 2:V_BIH + 3]).then_inc(s_ns, 1)
            run(act, step)

        @block.vector
        def _(dve):
            def step(s, k, first):
                dve.wait_ge(s_rs, s + 1)
                dve.wait_ge(s_n, s + 1)
                if first:
                    nc.vector.tensor_scalar(rn[:, k, :], r[:, k, :], vec[:, V_BHH + 2:V_BHH + 3], None, ALU.mult).then_inc(s_rn, 1)
                else:
                    nc.vector.scalar_tensor_tensor(rn[:, k, :], ps[:, 4 * k + 2, 0:B], vec[:, V_BHH + 2:V_BHH + 3], r[:, k, :],
                                                   ALU.add, ALU.mult).then_inc(s_rn, 1)
                dve.wait_ge(s_rn, s + 1)
                nc.vector.tensor_tensor(pre[:, k, :], rn[:, k, :], ps[:, 4 * k + 3, 0:B], ALU.add).then_inc(s_pre, 1)
                dve.wait_ge(s_zs, s + 1)
                if first:
                    nc.vector.memset(zh[:, k, :], 0.0).then_inc(s_zh, 1)
                else:
                    dve.wait_ge(s_h, s)
                    nc.vector.tensor_tensor(zh[:, k, :], z[:, k, :], hist[:, bass.ds(s - 1, 1), :].rearrange("p o b -> p (o b)"),
                                            ALU.mult).then_inc(s_zh, 1)
                nc.vector.tensor_scalar(omz[:, k, :], z[:, k, :], -1.0, 1.0, ALU.mult, ALU.add).then_inc(s_omz, 1)
                dve.wait_ge(s_omz, s + 1)
                dve.wait_ge(s_ns, s + 1)
                nc.vector.tensor_tensor(m[:, k, :], omz[:, k, :], n[:, k, :], ALU.mult).then_inc(s_m, 1)
                dve.wait_ge(s_zh, s + 1)
                dve.wait_ge(s_m, s + 1)
                nc.vector.tensor_tensor(hist[:, bass.ds(s, 1), :].rearrange("p o b -> p (o b)"), m[:, k, :], zh[:, k, :],
                                        ALU.add).then_inc(s_h, 1)
            run(dve, step)


def turn_and_fold(nc, col, states, hist, keymat, ps):
    with nc.semaphore("b_key_product") as s_mm, nc.semaphore("b_copied") as s_cp, nc.Block() as block:
        @block.tensor
        def _(pe):
            for k in range(4):
                last = nc.tensor.matmul(ps[0:64, k, 0:256], col["wqpkT"][:, k * 64:(k + 1) * 64],
                                        col["keys"][:, k * 256:(k + 1) * 256], start=True, stop=True)
            last.then_inc(s_mm, 1)

        @block.scalar
        def _(act):
            nc.scalar.copy(hist[0:64].rearrange("p t b -> p (t b)"), states[0:64].rearrange("p t b -> p (t b)")).then_inc(s_cp, 1)
            act.wait_ge(s_mm, 1)
            nc.scalar.copy(keymat[:].rearrange("p (k n) -> p k n", k=4), ps[0:64, 0:4, 0:256]).then_inc(s_cp, 1)
            act.wait_ge(s_cp, 3)

        @block.vector
        def _(dve):
            nc.vector.tensor_copy(hist[64:128], states[64:128, ::-1, :]).then_inc(s_cp, 1)
            dve.wait_ge(s_cp, 3)


def attention(nc, cst, keymat, table, out, resid, hist, ps):
    vec = cst["vecs"]
    ident = cst["ident"]
    with ExitStack() as ctx:
        def sb(name, shape, dt=F32):
            return ctx.enter_context(nc.sbuf_tensor(name, shape, dt))

        def sem(name):
            return ctx.enter_context(nc.semaphore(name))

        rows = sb("rows", [128, TT, 2 * D])
        wmat = sb("wmat", [128, TT, H])
        wT = sb("wT", [128, NT, TT])
        idxT = sb("idxT", [128, NT, TT], U32)
        kvT = sb("kvT", [128, H, T])
        vout = sb("vout", [TT, NT, H * D])
        resb = sb("resb", [64, T])
        gate = sb("gate", [64, T])
        mix = sb("mix", [64, T])
        cen = sb("cen", [64, T])
        pre_h, pre_u = sb("pre_h", [64, T]), sb("pre_u", [64, T])
        cur_h, cur_u = sb("cur_h", [64, T]), sb("cur_u", [64, T])
        sc = sb("sc", [TT, 16, NK])
        top = sb("top", [TT, 16, K])
        topi = sb("topi", [TT, 16, K], U32)
        topf = sb("topf", [TT, 16, K])
        cs = sb("cs", [TT, H, CAND])
        ci = sb("ci", [TT, H, CAND])
        fin = sb("fin", [TT, H, K])
        posi = sb("posi", [TT, H, K], U32)
        posf = sb("posf", [TT, H, K])
        hot = sb("hot", [TT, 2, K, CAND])
        idxf = sb("idxf", [TT, H, K])
        ew = sb("ew", [TT, H, K])
        esum = sb("esum", [TT, H])
        qt = sb("qt", [64, H, TT])
        sm = sb("sm", [TT, 2, T])
        prob = sb("prob", [TT, 2, T])
        probT = sb("probT", [TT, T])
        dg = sb("dg", [TT, 2, TT])
        mx = sb("mx", [TT, 4, H])
        osb = sb("osb", [TT, D])

        s_rb = sem("c_resid_loaded")
        s_p1, s_pg, s_pt, s_po, s_ph = (sem(n) for n in ("c_gate_products", "c_gate", "c_mix", "c_out_product", "c_h"))
        s_pm, s_pc, s_pq, s_pv, s_psd, s_pu = (sem(n) for n in ("c_mean", "c_centred", "c_squared", "c_variance", "c_deviation", "c_u"))
        s_passed = sem("c_passed")
        s_chain = sem("c_pre_vector_chain")
        s_cur = sem("c_row_promoted")
        s_fs, s_fsc, s_fk = sem("c_score_product"), sem("c_scores_copied"), sem("c_scores_used")
        s_fd = sem("c_front_vector_chain")
        s_hot = sem("c_one_hot_chain")
        s_few, s_fexp = sem("c_exponents_ready"), sem("c_exponentials")
        s_fi, s_ft, s_fT = sem("c_indices_and_weights"), sem("c_turned"), sem("c_turned_copied")
        s_g = [sem(f"c_gathered{g}") for g in range(NG)]
        s_wm, s_rf, s_ke = sem("c_weight_matrix"), sem("c_row_slots_used"), sem("c_kv_copied")
        s_av, s_avc, s_aq, s_aqc = sem("c_vout_product"), sem("c_vout_copied"), sem("c_q_product"), sem("c_q_copied")
        s_s, s_sm, s_nm, s_e = sem("c_sim"), sem("c_sim_masked"), sem("c_max_negated"), sem("c_exp")
        s_ri, s_dg, s_tp, s_tpc = sem("c_sum_inverted"), sem("c_scaled_identity"), sem("c_probs_turned"), sem("c_probs_copied")
        s_o, s_osb, s_out = sem("c_out_summed"), sem("c_out_copied"), sem("c_out_stored")

        block = ctx.enter_context(nc.Block())

        def run(eng, pre, front, promote, tile):
            pre(0)
            for c in range(NT):
                front(c, 0, c)
            with eng.Fori(0, B - 1) as n:
                promote(n)
                for c in range(NT):
                    tile(n * NT + c, n, c, n * NT + (c + NT))
                    if c == 0:
                        pre(n + 1)
                    front(n * NT + (c + NT), n + 1, c)
            promote(B - 1)
            for c in range(NT):
                tile((B - 1) * NT + c, B - 1, c, B * NT)

        def settle(eng):
            eng.sem_inc(s_passed, 1)

        @block.sync
        def _(sp):
            sp.dma_start(resb[:], resid[0]).then_inc(s_rb, 16)

            def stores(n):
                for c in range(NT):
                    sp.wait_ge(s_osb, n * NT + (c + 2))
                    dst = out[bass.ds(n, 1), c * TT:(c + 1) * TT, :] if not isinstance(n, int) else out[n:n + 1, c * TT:(c + 1) * TT, :]
                    sp.dma_start(dst.rearrange("o t d -> (o t) d"), osb[:]).then_inc(s_out, 16)

            with sp.Fori(0, B - 1) as n:
                sp.wait_ge(s_ph, n + 1)
                sp.dma_start(resb[:], resid[bass.ds(n + 1, 1)].rearrange("o d t -> (o d) t")).then_inc(s_rb, 16)
                stores(n)
            stores(B - 1)
            sp.wait_ge(s_out, 16 * (B * NT + 1))

        @block.gpsimd
        def _(pool):
            with pool.Fori(0, B) as n:
                for c in range(NT):
                    pool.wait_ge(s_fT, n * NT + (c + 1))
                    for g in range(NG):
                        pool.wait_ge(s_rf, n * (NT * NG) + (c * NG + g + 1))
                        settle(pool)
                        for t in range(g * GROUP, (g + 1) * GROUP):
                            nc.gpsimd.indirect_dma_start(
                                out=rows[:, t, :], out_offset=None, in_=table[:, :],
                                in_offset=bass.IndirectOffsetOnAxis(ap=idxT[:, c, t:t + 1], axis=0),
                            ).then_inc(s_g[g], 16)

        @block.tensor
        def _(pe):
            def mm(out_, lhsT, rhs, start=True, stop=True):
                return nc.tensor.matmul(out_, lhsT, rhs, start=start, stop=stop)

            nc.tensor.nop().then_inc(s_rf, NG)

            def pre(b):
                hb = hist[:, :, bass.ds(b, 1)] if not isinstance(b, int) else hist[:, :, b:b + 1]
                hb = hb.rearrange("p t o -> p (t o)")
                mm(ps[0:64, 2, 0:T], cst["gatew"], hb)
                mm(ps[0:64, 3, 0:T], cst["diff"], hb)
                mm(ps[0:64, 4, 0:T], cst["pickrev"], hb).then_inc(s_p1, 1)
                pe.wait_ge(s_pt, b + 1)
                settle(pe)
                mm(ps[0:64, 5, 0:T], cst["outw"][0:64], mix[:]).then_inc(s_po, 1)
                pe.wait_ge(s_ph, b + 1)
                settle(pe)
                mm(ps[0:64, 2, 0:T], cst["mean"][0:64, 0:64], pre_h[:]).then_inc(s_pm, 1)
                pe.wait_ge(s_pq, b + 1)
                settle(pe)
                mm(ps[0:64, 3, 0:T], cst["mean"][0:64, 0:64], gate[:]).then_inc(s_pv, 1)

            def front(f, b, c):
                pe.wait_ge(s_pu, b + 1)
                if not (isinstance(f, int) and f == 0):
                    pe.wait_ge(s_fT, f)
                mm(ps[0:TT, 2, :], pre_u[:, c * TT:(c + 1) * TT], keymat[:, 0:512])
                mm(ps[0:TT, 3, :], pre_u[:, c * TT:(c + 1) * TT], keymat[:, 512:1024]).then_inc(s_fs, 1)
                pe.wait_ge(s_fi, f + 1)
                nc.tensor.transpose(ps[:, 2, 0:TT], idxf[:].rearrange("p h k -> p (h k)"), ident[0:TT, 0:TT])
                nc.tensor.transpose(ps[:, 2, 128:128 + TT], ew[:].rearrange("p h k -> p (h k)"),
                                    ident[0:TT, 0:TT]).then_inc(s_ft, 1)

            def promote(n):
                pass

            def tile(q, n, c, fronts):
                pe.wait_ge(s_wm, q + 1)
                pe.wait_ge(s_ke, q + 1)
                for g in range(NG):
                    pe.wait_ge(s_g[g], (q + 1) * (16 * GROUP))
                    for t in range(g * GROUP, (g + 1) * GROUP):
                        last = mm(ps[:, t // 64, (t % 64) * H:(t % 64 + 1) * H], rows[:, t, :], wmat[:, t, :])
                    last.then_inc(s_rf, 1)
                pe.wait_ge(s_ke, q + 2)
                for h in range(H):
                    last = mm(ps[0:TT, 6, h * D:(h + 1) * D], kvT[64:128, h, c * TT:(c + 1) * TT],
                              cst["wo"][64:128, h * D:(h + 1) * D])
                last.then_inc(s_av, 1)
                pe.wait_ge(s_cur, n + 1)
                pe.wait_ge(s_fT, fronts)
                settle(pe)
                for h in range(H):
                    last = mm(ps[0:64, 2 + h // 4, (h % 4) * TT:(h % 4 + 1) * TT], cst["wq"][0:64, h * D:(h + 1) * D],
                              cur_u[:, c * TT:(c + 1) * TT])
                last.then_inc(s_aq, 1)
                pe.wait_ge(s_aqc, q + 1)

                def sim(h):
                    if h >= 2:
                        pe.wait_ge(s_sm, q * H + (h - 1))
                    mm(ps[0:TT, 4 + h % 2, 0:(c + 1) * TT], qt[:, h, :], kvT[0:64, h, 0:(c + 1) * TT]).then_inc(s_s, 1)

                sim(0)
                for h in range(H):
                    if h + 1 < H:
                        sim(h + 1)
                    pe.wait_ge(s_dg, q * H + (h + 1))
                    if h == 0:
                        pe.wait_ge(s_avc, q + 1)
                    for j in range(c + 1):
                        last = mm(ps[0:TT, 6, j * TT:(j + 1) * TT], prob[:, h % 2, j * TT:(j + 1) * TT], dg[:, h % 2, :])
                    last.then_inc(s_tp, 1)
                    pe.wait_ge(s_tpc, q * H + (h + 1))
                    if h == 0:
                        pe.wait_ge(s_osb, q + 1)
                    for j in range(c + 1):
                        mm(ps[0:TT, 7, 0:D], probT[:, j * TT:(j + 1) * TT], vout[:, j, h * D:(h + 1) * D],
                           start=(h == 0 and j == 0), stop=False)
                mm(ps[0:TT, 7, 0:D], cur_h[:, c * TT:(c + 1) * TT], ident[0:64, 0:D], start=False).then_inc(s_o, 1)

            run(pe, pre, front, promote, tile)

        @block.scalar
        def _(act):
            def pre(b):
                act.wait_ge(s_p1, b + 1)
                nc.scalar.activation(gate[:], ps[0:64, 2, 0:T], ACT.Sigmoid, bias=vec[0:64, V_GATEB:V_GATEB + 1]).then_inc(s_pg, 1)
                act.wait_ge(s_pc, b + 1)
                nc.scalar.activation(gate[:], cen[:], ACT.Square).then_inc(s_pq, 1)
                act.wait_ge(s_pv, b + 1)
                nc.scalar.activation(mix[:], ps[0:64, 3, 0:T], ACT.Sqrt, bias=vec[0:64, V_EPS:V_EPS + 1]).then_inc(s_psd, 1)

            def front(f, b, c):
                act.wait_ge(s_fs, f + 1)
                if not (isinstance(f, int) and f == 0):
                    act.wait_ge(s_fk, f)
                flat = sc[:].rearrange("p g k -> p (g k)")
                nc.scalar.copy(flat[:, 0:512], ps[0:TT, 2, :])
                nc.scalar.copy(flat[:, 512:1024], ps[0:TT, 3, :]).then_inc(s_fsc, 1)
                act.wait_ge(s_few, f + 1)
                nc.scalar.activation(ew[:], ew[:], ACT.Exp).then_inc(s_fexp, 1)

            def promote(n):
                act.wait_ge(s_pu, n + 1)
                if not isinstance(n, int):
                    act.wait_ge(s_o, n * NT + 1)
                else:
                    act.wait_ge(s_o, n * NT + 1)
                nc.scalar.copy(cur_h[:], pre_h[:])
                nc.scalar.copy(cur_u[:], pre_u[:]).then_inc(s_cur, 1)

            def tile(q, n, c, fronts):
                act.wait_ge(s_rf, q * NG + 2 * NG)
                dst = kvT[:, :, c * TT:(c + 1) * TT]
                nc.scalar.copy(dst[:, :, 0:64], ps[:, 0, :].rearrange("p (t h) -> p h t", h=H))
                nc.scalar.copy(dst[:, :, 64:TT], ps[:, 1, 0:(TT - 64) * H].rearrange("p (t h) -> p h t", h=H)).then_inc(s_ke, 1)
                act.wait_ge(s_av, q + 1)
                nc.scalar.copy(vout[:, c, :], ps[0:TT, 6, :]).then_inc(s_avc, 1)
                act.wait_ge(s_aq, q + 1)
                for j in range(2):
                    last = nc.scalar.mul(qt[:, 4 * j:4 * j + 4, :], ps[0:64, 2 + j, 0:4 * TT].rearrange("p (h t) -> p h t", h=4), D ** -0.5)
                last.then_inc(s_aqc, 1)
                J = (c + 1) * TT
                for h in range(H):
                    act.wait_ge(s_nm, q * H + (h + 1))
                    if h >= 2:
                        act.wait_ge(s_tp, q * H + (h - 1))
                    nc.scalar.activation(prob[:, h % 2, 0:J], sm[:, h % 2, 0:J], ACT.Exp, bias=mx[:, 1, h:h + 1],
                                         accum_out=mx[:, 2, h:h + 1]).then_inc(s_e, 1)
                    act.wait_ge(s_tp, q * H + (h + 1))
                    nc.scalar.copy(probT[:, 0:J], ps[0:TT, 6, 0:J]).then_inc(s_tpc, 1)
                act.wait_ge(s_o, q + 2)
                act.wait_ge(s_out, q * 16 + 16)
                nc.scalar.copy(osb[:], ps[0:TT, 7, 0:D]).then_inc(s_osb, 1)

            run(act, pre, front, promote, tile)

        @block.vector
        def _(dve):
            nc.vector.nop().then_inc(s_ke, 1)
            nc.vector.nop().then_inc(s_osb, 1)
            nc.vector.nop().then_inc(s_o, 1)
            nc.vector.nop().then_inc(s_out, 16)

            def pre(b):
                dve.wait_ge(s_pg, b + 1)
                nc.vector.tensor_tensor(mix[:], gate[:], ps[0:64, 3, 0:T], ALU.mult).then_inc(s_chain, 1)
                dve.wait_ge(s_chain, b * 3 + 1)
                nc.vector.tensor_tensor(mix[:], mix[:], ps[0:64, 4, 0:T], ALU.add).then_inc(s_pt, 1)
                dve.wait_ge(s_po, b + 1)
                dve.wait_ge(s_rb, b * 16 + 16)
                if not (isinstance(b, int) and b == 0):
                    dve.wait_ge(s_cur, b)
                nc.vector.scalar_tensor_tensor(pre_h[:], ps[0:64, 5, 0:T], vec[0:64, V_OUTB:V_OUTB + 1], resb[:],
                                               ALU.add, ALU.add).then_inc(s_ph, 1)
                dve.wait_ge(s_ph, b + 1)
                dve.wait_ge(s_pm, b + 1)
                nc.vector.tensor_tensor(cen[:], pre_h[:], ps[0:64, 2, 0:T], ALU.subtract).then_inc(s_pc, 1)
                dve.wait_ge(s_psd, b + 1)
                nc.vector.reciprocal(mix[:], mix[:]).then_inc(s_chain, 1)
                dve.wait_ge(s_pc, b + 1)
                dve.wait_ge(s_chain, b * 3 + 2)
                nc.vector.tensor_tensor(pre_u[:], cen[:], mix[:], ALU.mult).then_inc(s_pu, 1)
                nc.vector.nop().then_inc(s_chain, 1)

            LINKS = 18

            def front(f, b, c):
                count = [0]

                def link(ins):
                    count[0] += 1
                    ins.then_inc(s_fd, 1)
                    dve.wait_ge(s_fd, f * LINKS + count[0])

                def top16(values, best, where, groups):
                    settle(dve)
                    for g in range(groups):
                        last = nc.vector.max(best[:, g, 0:8], values[:, g, :])
                    link(last)
                    settle(dve)
                    for g in range(groups):
                        nc.vector.max_index(where[:, g, 0:8], best[:, g, 0:8], values[:, g, :])
                    for g in range(groups):
                        last = nc.vector.match_replace(values[:, g, :], best[:, g, 0:8], values[:, g, :], LOWEST)
                    link(last)
                    settle(dve)
                    for g in range(groups):
                        last = nc.vector.max(best[:, g, 8:16], values[:, g, :])
                    link(last)
                    settle(dve)
                    for g in range(groups):
                        last = nc.vector.max_index(where[:, g, 8:16], best[:, g, 8:16], values[:, g, :])
                    return last

                dve.wait_ge(s_fsc, f + 1)
                top16(sc, top, topi, 16).then_inc(s_fk, 1)
                dve.wait_ge(s_fk, f + 1)
                link(nc.vector.tensor_copy(topf[:], topi[:]))
                nc.vector.tensor_tensor(topf[:, 0:H, :], topf[:, 0:H, :],
                                        cst["headoff"][0:TT].unsqueeze(2).broadcast_to([TT, H, K]), ALU.add)
                link(nc.vector.tensor_scalar(topf[:, H:, :], topf[:, H:, :], float(NK), None, ALU.mult))
                for src, dst in ((top, cs), (topf, ci)):
                    at = 0
                    for a, na, nb in SEGMENTS:
                        o = dst[:, :, at:at + na * nb]
                        x0, x1 = src[:, 0:H, a:a + na], src[:, H:2 * H, 0:nb]
                        if na > 1 and nb > 1:
                            o = o.rearrange("p h (a b) -> p h a b", b=nb)
                            x0 = x0.unsqueeze(3).broadcast_to([TT, H, na, nb])
                            x1 = x1.unsqueeze(2).broadcast_to([TT, H, na, nb])
                        elif nb > 1:
                            x0 = x0.broadcast_to([TT, H, nb])
                        else:
                            x1 = x1.broadcast_to([TT, H, na])
                        last = nc.vector.tensor_tensor(o, x0, x1, ALU.add)
                        at += na * nb
                link(last)
                link(top16(cs, fin, posi, H))
                nc.vector.tensor_tensor(ew[:], fin[:], fin[:, :, 0:1].broadcast_to([TT, H, K]), ALU.subtract).then_inc(s_few, 1)
                link(nc.vector.tensor_copy(posf[:], posi[:]))
                for h in range(0, H, 2):
                    nc.vector.tensor_tensor(hot[:], posf[:, h:h + 2, :].unsqueeze(3).broadcast_to([TT, 2, K, CAND]),
                                            cst["iota"][0:TT].unsqueeze(1).unsqueeze(1).broadcast_to([TT, 2, K, CAND]),
                                            ALU.is_equal).then_inc(s_hot, 1)
                    dve.wait_ge(s_hot, f * 12 + (3 * (h // 2) + 1))
                    nc.vector.tensor_tensor(hot[:], hot[:], ci[:, h:h + 2, :].unsqueeze(2).broadcast_to([TT, 2, K, CAND]),
                                            ALU.mult).then_inc(s_hot, 1)
                    dve.wait_ge(s_hot, f * 12 + (3 * (h // 2) + 2))
                    nc.vector.tensor_reduce(idxf[:, h:h + 2, :], hot[:], AX_X, ALU.add).then_inc(s_hot, 1)
                    dve.wait_ge(s_hot, f * 12 + (3 * (h // 2) + 3))
                dve.wait_ge(s_fexp, f + 1)
                link(nc.vector.tensor_reduce(esum[:], ew[:], AX_X, ALU.add))
                link(nc.vector.reciprocal(esum[:], esum[:]))
                nc.vector.tensor_tensor(ew[:], ew[:], esum[:].unsqueeze(2).broadcast_to([TT, H, K]), ALU.mult).then_inc(s_fi, 1)
                while count[0] < LINKS:
                    count[0] += 1
                    nc.vector.nop().then_inc(s_fd, 1)
                dve.wait_ge(s_ft, f + 1)
                if isinstance(b, int) is False:
                    dve.wait_ge(s_rf, f * NG - (NT - 2) * NG)
                nc.vector.tensor_copy(idxT[:, c, :], ps[:, 2, 0:TT])
                nc.vector.tensor_copy(wT[:, c, :], ps[:, 2, 128:128 + TT]).then_inc(s_fT, 1)

            def promote(n):
                pass

            def tile(q, n, c, fronts):
                dve.wait_ge(s_rf, q * NG + NG)
                dve.wait_ge(s_fT, fronts)
                nc.vector.tensor_tensor(wmat[:], wT[:, c, :].unsqueeze(2).broadcast_to([128, TT, H]),
                                        cst["mask8"].unsqueeze(1).broadcast_to([128, TT, H]), ALU.mult).then_inc(s_wm, 1)
                J = (c + 1) * TT
                mask = cst["causal"][0:TT, T - c * TT:T + TT]

                def scaled_identity(h):
                    dve.wait_ge(s_e, q * H + (h + 1))
                    nc.vector.reciprocal(mx[:, 3, h:h + 1], mx[:, 2, h:h + 1]).then_inc(s_ri, 1)
                    dve.wait_ge(s_ri, q * H + (h + 1))
                    if h >= 2:
                        dve.wait_ge(s_tp, q * H + (h - 1))
                    nc.vector.tensor_scalar(dg[:, h % 2, :], ident[0:TT, 0:TT], mx[:, 3, h:h + 1], None,
                                            ALU.mult).then_inc(s_dg, 1)

                for h in range(H):
                    dve.wait_ge(s_s, q * H + (h + 1))
                    if h >= 2:
                        dve.wait_ge(s_e, q * H + (h - 1))
                    settle(dve)
                    nc.vector.tensor_tensor_reduce(sm[:, h % 2, 0:J], ps[0:TT, 4 + h % 2, 0:J], mask, 1.0, LOWEST,
                                                   ALU.add, ALU.max, mx[:, 0, h:h + 1]).then_inc(s_sm, 1)
                    dve.wait_ge(s_sm, q * H + (h + 1))
                    nc.vector.tensor_scalar(mx[:, 1, h:h + 1], mx[:, 0, h:h + 1], -1.0, None, ALU.mult).then_inc(s_nm, 1)
                    if h >= 1:
                        scaled_identity(h - 1)
                scaled_identity(H - 1)

            run(dve, pre, front, promote, tile)


def kernel(**inputs):
    from concourse.bacc import Bacc
    from concourse.bass_utils import run_bass_kernel_spmd

    pack, early = pack_constants(inputs)
    table = np.concatenate([inputs["L0_ffn_keys_table"], inputs["L0_ffn_values_table"]], axis=1)
    arrays = {"x_dram": np.ascontiguousarray(inputs["x"]), "pack_dram": pack, "early_dram": early,
              "table_dram": np.ascontiguousarray(table)}
    nc = Bacc("TRN2", target_bir_lowering=False, num_devices=1)
    args = [nc.dram_tensor(name, a.shape, mybir.dt.from_np(a.dtype), kind="ExternalInput").ap()
            for name, a in arrays.items()]
    result = nc.dram_tensor("out_dram", (B, T, D), F32, kind="ExternalOutput").ap()
    build(nc, *args, result)
    r = run_bass_kernel_spmd(nc, [arrays], core_ids=[0])
    return r.results[0]["out_dram"]


def pack_constants(inputs):
    w = {k[3:]: np.asarray(v) for k, v in inputs.items() if k != "x"}

    def two(a, b):
        z = np.zeros((128, 128), np.float32)
        z[0:64, 0:64], z[64:, 64:] = a, b
        return z

    def low(a):
        z = np.zeros((128, a.shape[1]), np.float32)
        z[0:a.shape[0]] = a
        return z

    def both(v):
        return np.concatenate([v, v])[:, None]

    f = {"ident": np.eye(128, dtype=np.float32)}
    f["mean"] = two(np.full((64, 64), 1 / 64, np.float32), np.full((64, 64), 1 / 64, np.float32))
    f["win0"] = two(w["tok_W_in"][0], w["tok_W_in"][0])
    f["win1"] = two(w["tok_W_in"][1], w["tok_W_in"][1])
    f["wout1"] = two(w["tok_W_out"][1], w["tok_W_out"][1])
    f["wout0"] = two(w["tok_W_out"][0], w["tok_W_out"][0])
    vec = [both(w["tok_b_in"][0]), both(w["tok_b_in"][1]), both(w["tok_b_out"][1]), both(w["tok_b_out"][0]),
           both(w["tok_core_diag"]), both(w["attn_ln_g"]), both(w["attn_ln_b"]),
           np.broadcast_to(w["tok_conv_filter"], (128, TAPS))]
    for side in ("ih", "hh"):
        for g in range(3):
            vec.append(np.concatenate([w[f"attn_fwd_b_{side}"][g * 64:(g + 1) * 64],
                                       w[f"attn_rev_b_{side}"][g * 64:(g + 1) * 64]])[:, None])
    vec += [low(w["attn_gate_b"][:, None]), low(w["attn_out_b"][:, None]),
            np.full((128, 1), EPS, np.float32)]
    f["vecs"] = np.concatenate(vec, axis=1)
    for side in ("ih", "hh"):
        f["w" + side] = np.concatenate(
            [two(w[f"attn_fwd_w_{side}"][g * 64:(g + 1) * 64].T, w[f"attn_rev_w_{side}"][g * 64:(g + 1) * 64].T)
             for g in range(3)], axis=1)
    f["gatew"] = w["attn_gate_w"].T
    eye = np.eye(64, dtype=np.float32)
    f["diff"] = np.concatenate([eye, -eye])
    f["pickrev"] = np.concatenate([0 * eye, eye])
    f["outw"] = low(w["attn_out_w"].T)
    f["mask8"] = np.repeat(np.eye(H, dtype=np.float32), K, axis=0)
    f["iota"] = np.broadcast_to(np.arange(CAND, dtype=np.float32), (128, CAND))
    tri = np.where(np.arange(128)[:, None] >= np.arange(TT)[None], 0.0, LOWEST).astype(np.float32)
    f["causal"] = np.concatenate([np.zeros((128, T), np.float32), tri], axis=1)
    f["headoff"] = np.broadcast_to(np.arange(H, dtype=np.float32) * NK * NK, (128, H))
    qpk = w["ffn_Wq_pk"].T.reshape(4, 128, 64)
    f["wqpkT"] = np.concatenate(list(qpk), axis=1)
    keys = np.zeros((2, 2, 4, 32, 4, 64), np.float32)
    for h in range(4):
        keys[:, :, h, :, h, :] = w["ffn_pk_keys"].reshape(2, 64, 2, 4, 32)[:, :, :, h].transpose(0, 2, 3, 1)
    f["keys"] = np.concatenate(list(keys.reshape(4, 128, 256)), axis=1)
    f["wq"] = low(w["ffn_Wq"])
    wo = np.zeros((128, 512), np.float32)
    wo[64:] = w["ffn_Wo"].reshape(8, 64, 64).transpose(1, 0, 2).reshape(64, 512)
    f["wo"] = wo
    for name, width in FIELDS + EARLY:
        assert f[name].shape == (128, width), (name, f[name].shape)
    return [np.ascontiguousarray(np.concatenate([f[name] for name, _ in names], axis=1)) for names in (FIELDS, EARLY)]
```

```python
from contextlib import ExitStack

import numpy as np

import concourse.bass as bass
from concourse import mybir

ALU = mybir.AluOpType
ACT = mybir.ActivationFunctionType
AX_X = mybir.AxisListType.X
F32 = mybir.dt.float32
U32 = mybir.dt.uint32

B, T_IN, D = 16, 750, 64
TAPS, STRIDE = 15, 2
T = (T_IN - 1) // STRIDE + 1
PAD = TAPS // 2
PAIRS = B // 2
H, K, NK = 8, 16, 64
TT = 125
NT = T // TT
BLK = T_IN // TT
EPS = 1e-5
LOWEST = -3.0e38
HK = H * K
SEGMENTS = []
for _a in range(K):
    _nb = K // (_a + 1)
    if SEGMENTS and SEGMENTS[-1][2] == _nb:
        SEGMENTS[-1][1] += 1
    else:
        SEGMENTS.append([_a, 1, _nb])
CAND = sum(na * nb for _, na, nb in SEGMENTS)
GROUP = 5
NG = TT // GROUP

FIELDS = [
    ("ident", 128), ("mean", 128), ("vecs", 4 + 3 + TAPS + 3), ("gatew", 64), ("diff", 64),
    ("pickrev", 64), ("outw", 64), ("mask8", H), ("iota", CAND), ("causal", T + TT),
    ("headoff", H), ("wq", 512), ("wo", 512),
]
EARLY = [
    ("win0", 128), ("win1", 128), ("wout1", 128), ("wout0", 128), ("wih", 192), ("whh", 192),
    ("bih", 192), ("bhh", 192), ("dirsel", 2 * B), ("wqpkT", 256), ("keys", 1024),
]
WIDTH = sum(w for _, w in FIELDS)
EARLY_WIDTH = sum(w for _, w in EARLY)
V_BTOK, V_CORE, V_LNG, V_LNB, V_FILT = 0, 4, 5, 6, 7
V_GATEB = V_FILT + TAPS
V_OUTB = V_GATEB + 1
V_EPS = V_OUTB + 1


def fields(tensor, names):
    views, at = {}, 0
    for name, width in names:
        views[name] = tensor[:, at:at + width]
        at += width
    return views


def build(nc, x, pack, early, table, out):
    resid = nc.dram_tensor("resid", (B, D, T), F32).ap()
    with ExitStack() as ctx:
        cst = ctx.enter_context(nc.sbuf_tensor("cst", [128, WIDTH], F32))
        hist = ctx.enter_context(nc.sbuf_tensor("hist", [128, T, B], F32))
        keymat = ctx.enter_context(nc.sbuf_tensor("keymat", [64, 1024], F32))
        ps = ctx.enter_context(nc.psum_tensor("ps", [128, 8, 512], F32))
        col = fields(cst, FIELDS)
        with ExitStack() as until_gru:
            def sb(name, shape):
                return until_gru.enter_context(nc.sbuf_tensor(name, shape, F32))
            first = sb("early", [128, EARLY_WIDTH])
            core = sb("core", [128, 1])
            steps = sb("steps", [128, T, 2 * B])
            both = {**col, **fields(first, EARLY)}
            token_mixer(nc, x, (pack, early), (cst, first), both, core, steps, resid, ps)
            states = sb("states", [64, T, 2 * B])
            gru(nc, both, steps, states, ps)
            turn_and_fold(nc, both, states, hist, keymat, ps)
        attention(nc, col, keymat, table, out, resid, hist, ps)


def token_mixer(nc, x, packs, csts, col, core, steps, resid, ps):
    vec = col["vecs"]
    with ExitStack() as ctx:
        def sb(name, shape):
            return ctx.enter_context(nc.sbuf_tensor(name, shape, F32))

        def sem(name):
            return ctx.enter_context(nc.semaphore(name))

        xin = [sb(f"xin{u}", [TT, BLK, 2, 64]) for u in range(2)]
        xT = [sb(f"xT{u}", [128, T_IN]) for u in range(2)]
        one = [sb(f"layer_a{u}", [128, T_IN]) for u in range(2)]
        two = [sb(f"layer_b{u}", [128, T_IN]) for u in range(2)]
        padded = [sb(f"padded{u}", [128, T_IN + 2 * PAD]) for u in range(2)]
        hT = [sb(f"hT{u}", [128, T]) for u in range(2)]
        cen = [sb(f"cen{u}", [128, T]) for u in range(2)]
        sq = [sb(f"sq{u}", [128, T]) for u in range(2)]
        sd = [sb(f"sd{u}", [128, T]) for u in range(2)]
        nrm = [sb(f"nrm{u}", [128, T]) for u in range(2)]
        res = [sb(f"res{u}", [128, T]) for u in range(2)]
        xn = [sb(f"xn{u}", [128, T]) for u in range(2)]

        s_cst = sem("a_consts_loaded")
        s_x = [sem(f"a_x_loaded{u}") for u in range(2)]
        s_pad = sem("a_pads_zeroed")
        s_tr = sem("a_x_transposed")
        s_xT = sem("a_xT_copied")
        s_mm = sem("a_layer_product")
        s_th = sem("a_tanh_done")
        s_sq = sem("a_squared_by_core")
        s_stat = sem("a_statistic_product")
        s_dve = sem("a_vector_chain")
        s_cen = sem("a_centred")
        s_csq = sem("a_centred_squared")
        s_sd = sem("a_deviation")
        s_rec = sem("a_deviation_inverted")
        s_nrm = sem("a_normed")
        s_xn = sem("a_gru_input_ready")
        s_put = sem("a_gru_input_placed")
        s_put2 = sem("a_gru_input_placed_pool")
        s_res = [sem(f"a_resid_stored{u}") for u in range(2)]
        s_free = sem("a_resid_buffer_free")
        s_setup = sem("a_setup_done")

        block = ctx.enter_context(nc.Block())

        @block.sync
        def _(sp):
            for dst, src in zip(csts, packs):
                sp.dma_start(dst[:], src[:]).then_inc(s_cst, 16)
            with sp.Fori(0, PAIRS // 2) as g:
                for u in range(2):
                    sp.wait_ge(s_tr, g * 2 + (u + 1))
                    for half in range(2):
                        src = x[bass.ds(g * 2 + (u + 8 * half), 1)].rearrange("o (p k) d -> p (o k) d", k=BLK)
                        sp.dma_start(xin[u][:, :, half, :], src).then_inc(s_x[u], 16)

        @block.tensor
        def _(pe):
            pe.wait_ge(s_cst, 32)
            nc.tensor.nop().then_inc(s_tr, 2)
            banks = [ps[:, 4 * u:4 * u + 4, :] for u in range(2)]

            def layer(g, u, k, weight, src):
                for j in range(2):
                    mm = nc.tensor.matmul(banks[u][:, 2 + j, 0:T], weight, src[:, j * T:(j + 1) * T],
                                          start=True, stop=True)
                mm.then_inc(s_mm, 1)

            def stat(u, bank, src):
                nc.tensor.matmul(banks[u][:, bank, 0:T], col["mean"], src[:, :],
                                 start=True, stop=True).then_inc(s_stat, 1)

            with pe.Fori(0, PAIRS // 2) as g:
                for u in range(2):
                    pe.wait_ge(s_x[u], g * 32 + 32)
                    pe.wait_ge(s_xn, g * 2 + (u + 1))
                    for k in range(BLK):
                        tr = nc.tensor.transpose(banks[u][:, k // 3, (k % 3) * TT:(k % 3 + 1) * TT],
                                                 xin[u][:, k].rearrange("p a d -> p (a d)"), col["ident"][0:TT, 0:TT])
                    tr.then_inc(s_tr, 1)
                for u in range(2):
                    pe.wait_ge(s_xT, g * 2 + (u + 1))
                    layer(g, u, 0, col["win0"], xT[u])
                for u in range(2):
                    pe.wait_ge(s_th, g * 8 + (u + 1))
                    layer(g, u, 1, col["win1"], one[u])
                for u in range(2):
                    pe.wait_ge(s_sq, g * 2 + (u + 1))
                    layer(g, u, 2, col["wout1"], one[u])
                for u in range(2):
                    pe.wait_ge(s_th, g * 8 + (4 + u + 1))
                    layer(g, u, 3, col["wout0"], two[u])
                for u in range(2):
                    pe.wait_ge(s_nrm, g * 6 + (u + 1))
                    stat(u, 0, hT[u])
                for u in range(2):
                    pe.wait_ge(s_csq, g * 4 + (u + 1))
                    stat(u, 1, sq[u])
                for u in range(2):
                    pe.wait_ge(s_nrm, g * 6 + (2 + u + 1))
                    stat(u, 0, nrm[u])
                for u in range(2):
                    pe.wait_ge(s_csq, g * 4 + (2 + u + 1))
                    stat(u, 1, sq[u])

        @block.scalar
        def _(act):
            act.wait_ge(s_cst, 32)
            nc.scalar.activation(core[:], vec[:, V_CORE:V_CORE + 1], ACT.Abs).then_inc(s_setup, 1)
            act.wait_ge(s_pad, 4)
            with act.Fori(0, PAIRS // 2) as g:
                def tanh(g, u, k, dst):
                    act.wait_ge(s_mm, g * 8 + (2 * k + u + 1))
                    src = ps[:, 4 * u + 2:4 * u + 4, 0:T]
                    nc.scalar.activation(dst.rearrange("p (a b) -> p a b", a=2), src, ACT.Tanh,
                                         bias=vec[:, V_BTOK + k:V_BTOK + k + 1]).then_inc(s_th, 1)
                for u in range(2):
                    tanh(g, u, 0, one[u][:, :])
                for u in range(2):
                    tanh(g, u, 1, two[u][:, :])
                for u in range(2):
                    tanh(g, u, 2, two[u][:, :])
                for u in range(2):
                    act.wait_ge(s_cen, g * 4 + (u + 1))
                    tanh(g, u, 3, padded[u][:, PAD:PAD + T_IN])
                for v in range(2):
                    for u in range(2):
                        act.wait_ge(s_cen, g * 4 + (2 + 2 * v + u + 1))
                        nc.scalar.activation(sq[u][:, :], cen[u][:, :], ACT.Square).then_inc(s_csq, 1)
                    for u in range(2):
                        act.wait_ge(s_stat, g * 8 + (4 * v + 2 + u + 1))
                        nc.scalar.activation(sd[u][:, :], ps[:, 4 * u + 1, 0:T], ACT.Sqrt,
                                             bias=vec[:, V_EPS:V_EPS + 1]).then_inc(s_sd, 1)
                for u in range(2):
                    act.wait_ge(s_xn, g * 2 + (2 + u + 1))
                    nc.scalar.copy(steps[0:64, :, bass.ds(g * 2 + u, 1)], xn[u][0:64, :].unsqueeze(2))
                    nc.scalar.copy(steps[64:128, :, bass.ds(g * 2 + (u + B), 1)], xn[u][0:64, ::-1].unsqueeze(2))
                    nc.scalar.copy(steps[0:64, :, bass.ds(g * 2 + (u + 8), 1)], xn[u][64:128, :].unsqueeze(2)).then_inc(s_put, 1)

        @block.gpsimd
        def _(pool):
            for u in range(2):
                nc.gpsimd.memset(padded[u][:, 0:PAD], 0.0).then_inc(s_pad, 1)
                nc.gpsimd.memset(padded[u][:, PAD + T_IN:], 0.0).then_inc(s_pad, 1)
            with pool.Fori(0, PAIRS // 2) as g:
                for u in range(2):
                    pool.wait_ge(s_xn, g * 2 + (2 + u + 1))
                    nc.gpsimd.tensor_copy(steps[64:128, :, bass.ds(g * 2 + (u + 8 + B), 1)], xn[u][64:128, ::-1].unsqueeze(2)).then_inc(s_put2, 1)
                    for half in range(2):
                        pool.dma_start(resid[bass.ds(g * 2 + (u + 8 * half), 1)].rearrange("o d t -> (o d) t"),
                                       res[u][64 * half:64 * half + 64, :]).then_inc(s_res[u], 16)
                for u in range(2):
                    pool.wait_ge(s_res[u], g * 32 + 32)
                    pool.sem_inc(s_free, 1)

        @block.vector
        def _(dve):
            nc.vector.memset(steps[0:64, :, B:], 0.0)
            nc.vector.memset(steps[64:128, :, 0:B], 0.0)
            dve.wait_ge(s_cst, 32)
            dve.wait_ge(s_setup, 1)
            nc.vector.nop().then_inc(s_xn, 2)
            nc.vector.nop().then_inc(s_cen, 2)
            nc.vector.nop().then_inc(s_put, 2)
            nc.vector.nop().then_inc(s_put2, 2)
            nc.vector.nop().then_inc(s_free, 2)
            dve.wait_ge(s_pad, 4)
            with dve.Fori(0, PAIRS // 2) as g:
                for u in range(2):
                    dve.wait_ge(s_tr, g * 2 + (2 + u + 1))
                    for half in range(2):
                        cp = nc.vector.tensor_copy(
                            xT[u][:, :].rearrange("f (p k) -> f k p", k=BLK)[:, 3 * half:3 * half + 3],
                            ps[:, 4 * u + half, 0:T].rearrange("f (k p) -> f k p", k=3))
                    cp.then_inc(s_xT, 1)
                for u in range(2):
                    dve.wait_ge(s_th, g * 8 + (2 + u + 1))
                    nc.vector.scalar_tensor_tensor(one[u][:, :], two[u][:, :], core[:], two[u][:, :],
                                                   ALU.mult, ALU.mult).then_inc(s_sq, 1)
                for k in range(TAPS):
                    for u in range(2):
                        taps = padded[u][:, k:k + 2 * T - 1:STRIDE]
                        f = vec[:, V_FILT + k:V_FILT + k + 1]
                        done = s_nrm if k == TAPS - 1 else s_dve
                        if k == 0:
                            dve.wait_ge(s_th, g * 8 + (6 + u + 1))
                            nc.vector.tensor_scalar(hT[u][:, :], taps, f, None, ALU.mult).then_inc(done, 1)
                        else:
                            dve.wait_ge(s_dve, g * (2 * TAPS) + (2 * (k - 1) + u + 1))
                            nc.vector.scalar_tensor_tensor(hT[u][:, :], taps, f, hT[u][:, :],
                                                           ALU.mult, ALU.add).then_inc(done, 1)
                for v in range(2):
                    for u in range(2):
                        dve.wait_ge(s_stat, g * 8 + (4 * v + u + 1))
                        src = (hT, nrm)[v][u]
                        nc.vector.tensor_tensor(cen[u][:, :], src[:, :], ps[:, 4 * u, 0:T],
                                                ALU.subtract).then_inc(s_cen, 1)
                    for u in range(2):
                        dve.wait_ge(s_sd, g * 4 + (2 * v + u + 1))
                        nc.vector.reciprocal(sd[u][:, :], sd[u][:, :]).then_inc(s_rec, 1)
                    for u in range(2):
                        dve.wait_ge(s_cen, g * 4 + (2 + 2 * v + u + 1))
                        dve.wait_ge(s_rec, g * 4 + (2 * v + u + 1))
                        if v == 1:
                            dve.wait_ge(s_put, g * 2 + (u + 1))
                            dve.wait_ge(s_put2, g * 2 + (u + 1))
                        nc.vector.tensor_tensor((nrm, xn)[v][u][:, :], cen[u][:, :], sd[u][:, :],
                                                ALU.mult).then_inc(s_nrm, 1)
                    if v == 0:
                        for u in range(2):
                            dve.wait_ge(s_nrm, g * 6 + (2 + u + 1))
                            dve.wait_ge(s_free, g * 2 + (u + 1))
                            nc.vector.tensor_tensor(res[u][:, :], hT[u][:, :], nrm[u][:, :], ALU.add).then_inc(s_dve, 1)
                for u in range(2):
                    dve.wait_ge(s_nrm, g * 6 + (4 + u + 1))
                    dve.wait_ge(s_dve, g * (2 * TAPS) + (2 * TAPS - 2 + u + 1))
                    nc.vector.tensor_scalar(xn[u][:, :], xn[u][:, :], vec[:, V_LNG:V_LNG + 1], vec[:, V_LNB:V_LNB + 1],
                                            ALU.mult, ALU.add).then_inc(s_xn, 1)


UNROLL = 22


def gru(nc, col, steps, states, ps):
    N = 2 * B
    with ExitStack() as ctx:
        def sb(name, shape):
            return ctx.enter_context(nc.sbuf_tensor(name, shape, F32))

        def sem(name):
            return ctx.enter_context(nc.semaphore(name))

        r = sb("r", [64, 2, N])
        z = sb("z", [64, 2, N])
        omz = sb("one_minus_z", [64, 2, N])
        rn = sb("r_times_n", [64, 2, N])
        npre = sb("n_before_tanh", [64, 2, N])
        n = sb("n", [64, 2, N])
        m = sb("m", [64, 2, N])
        zh = sb("zh", [64, 2, N])
        hmov = sb("h_moving", [128, 2, N])
        s_r, s_n, s_z = sem("g_r_product"), sem("g_n_product"), sem("g_z_product")
        s_rs, s_zs, s_ns = sem("g_r_sigmoid"), sem("g_z_sigmoid"), sem("g_n_tanh")
        s_rn, s_pre = sem("g_r_times_n"), sem("g_n_before_tanh")
        s_omz, s_zh, s_m, s_h, s_st = sem("g_one_minus_z"), sem("g_zh"), sem("g_m"), sem("g_h"), sem("g_state")

        BF16 = mybir.dt.bfloat16
        total = sb("bias_sum", [128, 4, 64])
        left = sb("bias_left", [128, 4, 64])
        part = [ctx.enter_context(nc.sbuf_tensor(f"bias_part{i}", [128, 4, 64], BF16)) for i in range(3)]
        bias = ctx.enter_context(nc.sbuf_tensor("bias", [128, 4, 64], BF16))
        which = ctx.enter_context(nc.sbuf_tensor("which", [128, N], BF16))
        s_b = sem("g_bias_chain")
        BIAS_LINKS = 11
        wih = [col["wih"][:, g * 64:(g + 1) * 64] for g in range(3)]
        whh = [col["whh"][:, g * 64:(g + 1) * 64] for g in range(3)]
        block = ctx.enter_context(nc.Block())
        rounds = (T - 1) // UNROLL
        assert rounds * UNROLL == T - 1 and UNROLL % 2 == 0

        def run(eng, step):
            step(0, 0, True)
            with eng.Fori(0, rounds) as i:
                for j in range(UNROLL):
                    step(i * UNROLL + (j + 1), (j + 1) % 2, False)

        @block.tensor
        def _(pe):
            def step(s, k, first):
                xs = steps[:, bass.ds(s, 1), :].rearrange("p o b -> p (o b)")
                bank = [ps[0:64, 4 * k + q, 0:N] for q in range(4)]

                def add_bias(q):
                    return nc.tensor.matmul(bank[(0, 1, 3, 2)[q]], bias[:, q, :], which[:], start=True,
                                            stop=(first and q == 3))

                def add_input(q, gate, stop):
                    return nc.tensor.matmul(bank[q], wih[gate], xs, start=False, stop=stop)

                add_bias(2)
                add_input(3, 2, True)
                add_bias(0)
                mr = add_input(0, 0, first)
                mn = add_bias(3)
                add_bias(1)
                mz = add_input(1, 1, first)
                if first:
                    mr.then_inc(s_r, 1)
                    mn.then_inc(s_n, 1)
                    mz.then_inc(s_z, 1)
                    return
                pe.wait_ge(s_h, s * 2)
                nc.tensor.matmul(bank[0], whh[0], hmov[:, 1 - k, :], start=False, stop=True).then_inc(s_r, 1)
                nc.tensor.matmul(bank[2], whh[2], hmov[:, 1 - k, :], start=False, stop=True).then_inc(s_n, 1)
                nc.tensor.matmul(bank[1], whh[1], hmov[:, 1 - k, :], start=False, stop=True).then_inc(s_z, 1)
            pe.wait_ge(s_b, BIAS_LINKS)
            run(pe, step)

        @block.scalar
        def _(act):
            def step(s, k, first):
                act.wait_ge(s_r, s + 1)
                nc.scalar.activation(r[:, k, :], ps[0:64, 4 * k, 0:N], ACT.Sigmoid).then_inc(s_rs, 1)
                act.wait_ge(s_z, s + 1)
                nc.scalar.activation(z[:, k, :], ps[0:64, 4 * k + 1, 0:N], ACT.Sigmoid).then_inc(s_zs, 1)
                act.wait_ge(s_pre, s + 1)
                nc.scalar.activation(n[:, k, :], npre[:, k, :], ACT.Tanh).then_inc(s_ns, 1)
            run(act, step)

        @block.vector
        def _(dve):
            count = [0]

            def link(ins):
                count[0] += 1
                ins.then_inc(s_b, 1)
                dve.wait_ge(s_b, count[0])

            bih, bhh = (col[w].rearrange("p (g d) -> p g d", g=3) for w in ("bih", "bhh"))
            nc.vector.tensor_tensor(total[:, 0:2, :], bih[:, 0:2, :], bhh[:, 0:2, :], ALU.add)
            nc.vector.tensor_copy(total[:, 2, :], bih[:, 2, :])
            link(nc.vector.tensor_copy(total[:, 3, :], bhh[:, 2, :]))
            link(nc.vector.tensor_copy(part[0][:], total[:]))
            link(nc.vector.tensor_tensor(left[:], total[:], part[0][:], ALU.subtract))
            link(nc.vector.tensor_copy(part[1][:], left[:]))
            link(nc.vector.tensor_tensor(left[:], left[:], part[1][:], ALU.subtract))
            link(nc.vector.tensor_copy(part[2][:], left[:]))
            link(nc.vector.memset(bias[:], 0.0))
            for i in range(3):
                link(nc.vector.tensor_copy(bias[32 * i:32 * i + 32], part[i][32 * i:32 * i + 32]))
            nc.vector.memset(hmov[:], 0.0)
            link(nc.vector.tensor_copy(which[:], col["dirsel"]))
            assert count[0] == BIAS_LINKS

            def step(s, k, first):
                dve.wait_ge(s_rs, s + 1)
                dve.wait_ge(s_n, s + 1)
                nc.vector.tensor_tensor(rn[:, k, :], ps[0:64, 4 * k + 2, 0:N], r[:, k, :], ALU.mult).then_inc(s_rn, 1)
                dve.wait_ge(s_rn, s + 1)
                nc.vector.tensor_tensor(npre[:, k, :], rn[:, k, :], ps[0:64, 4 * k + 3, 0:N], ALU.add).then_inc(s_pre, 1)
                dve.wait_ge(s_zs, s + 1)
                nc.vector.tensor_scalar(omz[:, k, :], z[:, k, :], -1.0, 1.0, ALU.mult, ALU.add).then_inc(s_omz, 1)
                if first:
                    nc.vector.memset(zh[:, k, :], 0.0).then_inc(s_zh, 1)
                else:
                    dve.wait_ge(s_st, s)
                    nc.vector.tensor_tensor(zh[:, k, :], z[:, k, :], states[:, bass.ds(s - 1, 1), :].rearrange("p o b -> p (o b)"),
                                            ALU.mult).then_inc(s_zh, 1)
                dve.wait_ge(s_omz, s + 1)
                dve.wait_ge(s_ns, s + 1)
                nc.vector.tensor_tensor(m[:, k, :], omz[:, k, :], n[:, k, :], ALU.mult).then_inc(s_m, 1)
                dve.wait_ge(s_zh, s + 1)
                dve.wait_ge(s_m, s + 1)
                nc.vector.tensor_tensor(hmov[0:64, k, 0:B], m[:, k, 0:B], zh[:, k, 0:B], ALU.add).then_inc(s_h, 1)
                nc.vector.tensor_tensor(hmov[64:128, k, B:], m[:, k, B:], zh[:, k, B:], ALU.add).then_inc(s_h, 1)
                nc.vector.tensor_tensor(states[:, bass.ds(s, 1), :].rearrange("p o b -> p (o b)"), m[:, k, :], zh[:, k, :],
                                        ALU.add).then_inc(s_st, 1)
            run(dve, step)


def turn_and_fold(nc, col, states, hist, keymat, ps):
    with nc.semaphore("b_key_product") as s_mm, nc.semaphore("b_copied") as s_cp, nc.Block() as block:
        @block.tensor
        def _(pe):
            for k in range(4):
                last = nc.tensor.matmul(ps[0:64, k, 0:256], col["wqpkT"][:, k * 64:(k + 1) * 64],
                                        col["keys"][:, k * 256:(k + 1) * 256], start=True, stop=True)
            last.then_inc(s_mm, 1)

        @block.scalar
        def _(act):
            nc.scalar.copy(hist[0:64], states[:, :, 0:B]).then_inc(s_cp, 1)
            act.wait_ge(s_mm, 1)
            nc.scalar.copy(keymat[:].rearrange("p (k n) -> p k n", k=4), ps[0:64, 0:4, 0:256]).then_inc(s_cp, 1)
            act.wait_ge(s_cp, 3)

        @block.vector
        def _(dve):
            nc.vector.tensor_copy(hist[64:128], states[:, ::-1, B:]).then_inc(s_cp, 1)
            dve.wait_ge(s_cp, 3)


def attention(nc, cst, keymat, table, out, resid, hist, ps):
    vec = cst["vecs"]
    ident = cst["ident"]
    with ExitStack() as ctx:
        def sb(name, shape, dt=F32):
            return ctx.enter_context(nc.sbuf_tensor(name, shape, dt))

        def sem(name):
            return ctx.enter_context(nc.semaphore(name))

        rows = sb("rows", [128, TT, 2 * D])
        wmat = sb("wmat", [128, TT, H])
        wT = sb("wT", [128, NT, TT])
        idxT = sb("idxT", [128, NT, TT], U32)
        kvT = sb("kvT", [128, H, T])
        vout = sb("vout", [TT, NT, H * D])
        resb = sb("resb", [64, T])
        gate = sb("gate", [64, T])
        mix = sb("mix", [64, T])
        cen = sb("cen", [64, T])
        pre_h, pre_u = sb("pre_h", [64, T]), sb("pre_u", [64, T])
        cur_h, cur_u = sb("cur_h", [64, T]), sb("cur_u", [64, T])
        sc = sb("sc", [TT, 16, NK])
        top = sb("top", [TT, 16, K])
        topi = sb("topi", [TT, 16, K], U32)
        topf = sb("topf", [TT, 16, K])
        cs = sb("cs", [TT, H, CAND])
        ci = sb("ci", [TT, H, CAND])
        fin = sb("fin", [TT, H, K])
        posi = sb("posi", [TT, H, K], U32)
        posf = sb("posf", [TT, H, K])
        hot = sb("hot", [TT, 2, K, CAND])
        idxf = sb("idxf", [TT, H, K])
        ew = sb("ew", [TT, H, K])
        esum = sb("esum", [TT, H])
        qt = sb("qt", [64, H, TT])
        sm = sb("sm", [TT, 2, T])
        prob = sb("prob", [TT, 2, T])
        probT = sb("probT", [TT, T])
        dg = sb("dg", [TT, 2, TT])
        mx = sb("mx", [TT, 4, H])
        osb = sb("osb", [TT, D])

        s_rb = sem("c_resid_loaded")
        s_p1, s_pg, s_pt, s_po, s_ph = (sem(n) for n in ("c_gate_products", "c_gate", "c_mix", "c_out_product", "c_h"))
        s_pm, s_pc, s_pq, s_pv, s_psd, s_pu = (sem(n) for n in ("c_mean", "c_centred", "c_squared", "c_variance", "c_deviation", "c_u"))
        s_passed = sem("c_passed")
        s_chain = sem("c_pre_vector_chain")
        s_cur = sem("c_row_promoted")
        s_fs, s_fsc, s_fk = sem("c_score_product"), sem("c_scores_copied"), sem("c_scores_used")
        s_fd = sem("c_front_vector_chain")
        s_hot = sem("c_one_hot_chain")
        s_few, s_fexp = sem("c_exponents_ready"), sem("c_exponentials")
        s_fi, s_ft, s_fT = sem("c_indices_and_weights"), sem("c_turned"), sem("c_turned_copied")
        s_g = [sem(f"c_gathered{g}") for g in range(NG)]
        s_wm, s_rf, s_ke = sem("c_weight_matrix"), sem("c_row_slots_used"), sem("c_kv_copied")
        s_av, s_avc, s_aq, s_aqc = sem("c_vout_product"), sem("c_vout_copied"), sem("c_q_product"), sem("c_q_copied")
        s_s, s_sm, s_nm, s_e = sem("c_sim"), sem("c_sim_masked"), sem("c_max_negated"), sem("c_exp")
        s_ri, s_dg, s_tp, s_tpc = sem("c_sum_inverted"), sem("c_scaled_identity"), sem("c_probs_turned"), sem("c_probs_copied")
        s_o, s_osb, s_out = sem("c_out_summed"), sem("c_out_copied"), sem("c_out_stored")

        block = ctx.enter_context(nc.Block())

        def nothing(*_):
            pass

        def run(eng, pre, front, turn, weigh, promote, gathered, attend):
            pre(0)
            for c in range(NT):
                front(c, 0, c)
                if c < NT - 1:
                    turn(c, c)
                if c == 0:
                    weigh(0, 0)
            with eng.Fori(0, B - 1) as n:
                promote(n)
                for c in range(NT):
                    gathered(n * NT + c, c)
                    turn(n * NT + (c + NT - 1), (c + NT - 1) % NT)
                    weigh(n * NT + (c + 1), (c + 1) % NT)
                    attend(n * NT + c, n, c, n * NT + (c + NT))
                    if c == 0:
                        pre(n + 1)
                    front(n * NT + (c + NT), n + 1, c)
            promote(B - 1)
            for c in range(NT):
                gathered((B - 1) * NT + c, c)
                if c == 0:
                    turn(B * NT - 1, NT - 1)
                if c < NT - 1:
                    weigh((B - 1) * NT + c + 1, c + 1)
                attend((B - 1) * NT + c, B - 1, c, B * NT)

        def settle(eng):
            eng.sem_inc(s_passed, 1)

        @block.sync
        def _(sp):
            sp.dma_start(resb[:], resid[0]).then_inc(s_rb, 16)

            def stores(n):
                for c in range(NT):
                    sp.wait_ge(s_osb, n * NT + (c + 2))
                    dst = out[bass.ds(n, 1), c * TT:(c + 1) * TT, :] if not isinstance(n, int) else out[n:n + 1, c * TT:(c + 1) * TT, :]
                    sp.dma_start(dst.rearrange("o t d -> (o t) d"), osb[:]).then_inc(s_out, 16)

            with sp.Fori(0, B - 1) as n:
                sp.wait_ge(s_ph, n + 1)
                sp.dma_start(resb[:], resid[bass.ds(n + 1, 1)].rearrange("o d t -> (o d) t")).then_inc(s_rb, 16)
                stores(n)
            stores(B - 1)
            sp.wait_ge(s_out, 16 * (B * NT + 1))

        @block.gpsimd
        def _(pool):
            with pool.Fori(0, B) as n:
                for c in range(NT):
                    pool.wait_ge(s_fT, n * NT + (c + 1))
                    for g in range(NG):
                        pool.wait_ge(s_rf, n * (NT * NG) + (c * NG + g + 1))
                        settle(pool)
                        for t in range(g * GROUP, (g + 1) * GROUP):
                            nc.gpsimd.indirect_dma_start(
                                out=rows[:, t, :], out_offset=None, in_=table[:, :],
                                in_offset=bass.IndirectOffsetOnAxis(ap=idxT[:, c, t:t + 1], axis=0),
                            ).then_inc(s_g[g], 16)

        @block.tensor
        def _(pe):
            def mm(out_, lhsT, rhs, start=True, stop=True):
                return nc.tensor.matmul(out_, lhsT, rhs, start=start, stop=stop)

            nc.tensor.nop().then_inc(s_rf, NG)

            def pre(b):
                hb = hist[:, :, bass.ds(b, 1)] if not isinstance(b, int) else hist[:, :, b:b + 1]
                hb = hb.rearrange("p t o -> p (t o)")
                mm(ps[0:64, 2, 0:T], cst["gatew"], hb)
                mm(ps[0:64, 3, 0:T], cst["diff"], hb)
                mm(ps[0:64, 4, 0:T], cst["pickrev"], hb).then_inc(s_p1, 1)
                pe.wait_ge(s_pt, b + 1)
                settle(pe)
                mm(ps[0:64, 5, 0:T], cst["outw"][0:64], mix[:]).then_inc(s_po, 1)
                pe.wait_ge(s_ph, b + 1)
                settle(pe)
                mm(ps[0:64, 2, 0:T], cst["mean"][0:64, 0:64], pre_h[:]).then_inc(s_pm, 1)
                pe.wait_ge(s_pq, b + 1)
                settle(pe)
                mm(ps[0:64, 3, 0:T], cst["mean"][0:64, 0:64], gate[:]).then_inc(s_pv, 1)

            def front(f, b, c):
                pe.wait_ge(s_pu, b + 1)
                if not (isinstance(f, int) and f == 0):
                    pe.wait_ge(s_fT, f)
                mm(ps[0:TT, 2, :], pre_u[:, c * TT:(c + 1) * TT], keymat[:, 0:512])
                mm(ps[0:TT, 3, :], pre_u[:, c * TT:(c + 1) * TT], keymat[:, 512:1024]).then_inc(s_fs, 1)

            def turn(f, c):
                pe.wait_ge(s_fi, f + 1)
                nc.tensor.transpose(ps[:, 2, 0:TT], idxf[:].rearrange("p h k -> p (h k)"), ident[0:TT, 0:TT])
                nc.tensor.transpose(ps[:, 2, 128:128 + TT], ew[:].rearrange("p h k -> p (h k)"),
                                    ident[0:TT, 0:TT]).then_inc(s_ft, 1)

            def gathered(q, c):
                pe.wait_ge(s_wm, q + 1)
                pe.wait_ge(s_ke, q + 1)
                for g in range(NG):
                    pe.wait_ge(s_g[g], (q + 1) * (16 * GROUP))
                    for t in range(g * GROUP, (g + 1) * GROUP):
                        last = mm(ps[:, t // 64, (t % 64) * H:(t % 64 + 1) * H], rows[:, t, :], wmat[:, t, :])
                    last.then_inc(s_rf, 1)

            def attend(q, n, c, turned):
                pe.wait_ge(s_ke, q + 2)
                for h in range(H):
                    last = mm(ps[0:TT, 6, h * D:(h + 1) * D], kvT[64:128, h, c * TT:(c + 1) * TT],
                              cst["wo"][64:128, h * D:(h + 1) * D])
                last.then_inc(s_av, 1)
                pe.wait_ge(s_cur, n + 1)
                pe.wait_ge(s_fT, turned)
                settle(pe)
                for h in range(H):
                    last = mm(ps[0:64, 2 + h // 4, (h % 4) * TT:(h % 4 + 1) * TT], cst["wq"][0:64, h * D:(h + 1) * D],
                              cur_u[:, c * TT:(c + 1) * TT])
                last.then_inc(s_aq, 1)
                pe.wait_ge(s_aqc, q + 1)

                def sim(h):
                    if h >= 2:
                        pe.wait_ge(s_sm, q * H + (h - 1))
                    mm(ps[0:TT, 4 + h % 2, 0:(c + 1) * TT], qt[:, h, :], kvT[0:64, h, 0:(c + 1) * TT]).then_inc(s_s, 1)

                sim(0)
                for h in range(H):
                    if h + 1 < H:
                        sim(h + 1)
                    pe.wait_ge(s_dg, q * H + (h + 1))
                    if h == 0:
                        pe.wait_ge(s_avc, q + 1)
                    for j in range(c + 1):
                        last = mm(ps[0:TT, 6, j * TT:(j + 1) * TT], prob[:, h % 2, j * TT:(j + 1) * TT], dg[:, h % 2, :])
                    last.then_inc(s_tp, 1)
                    pe.wait_ge(s_tpc, q * H + (h + 1))
                    if h == 0:
                        pe.wait_ge(s_osb, q + 1)
                    for j in range(c + 1):
                        mm(ps[0:TT, 7, 0:D], probT[:, j * TT:(j + 1) * TT], vout[:, j, h * D:(h + 1) * D],
                           start=(h == 0 and j == 0), stop=False)
                mm(ps[0:TT, 7, 0:D], cur_h[:, c * TT:(c + 1) * TT], ident[0:64, 0:D], start=False).then_inc(s_o, 1)

            run(pe, pre, front, turn, nothing, nothing, gathered, attend)

        @block.scalar
        def _(act):
            def pre(b):
                act.wait_ge(s_p1, b + 1)
                nc.scalar.activation(gate[:], ps[0:64, 2, 0:T], ACT.Sigmoid, bias=vec[0:64, V_GATEB:V_GATEB + 1]).then_inc(s_pg, 1)
                act.wait_ge(s_pc, b + 1)
                nc.scalar.activation(gate[:], cen[:], ACT.Square).then_inc(s_pq, 1)
                act.wait_ge(s_pv, b + 1)
                nc.scalar.activation(mix[:], ps[0:64, 3, 0:T], ACT.Sqrt, bias=vec[0:64, V_EPS:V_EPS + 1]).then_inc(s_psd, 1)

            def front(f, b, c):
                act.wait_ge(s_fs, f + 1)
                if not (isinstance(f, int) and f == 0):
                    act.wait_ge(s_fk, f)
                flat = sc[:].rearrange("p g k -> p (g k)")
                nc.scalar.copy(flat[:, 0:512], ps[0:TT, 2, :])
                nc.scalar.copy(flat[:, 512:1024], ps[0:TT, 3, :]).then_inc(s_fsc, 1)
                act.wait_ge(s_few, f + 1)
                nc.scalar.activation(ew[:], ew[:], ACT.Exp).then_inc(s_fexp, 1)

            def promote(n):
                act.wait_ge(s_pu, n + 1)
                act.wait_ge(s_o, n * NT + 1)
                nc.scalar.copy(cur_h[:], pre_h[:])
                nc.scalar.copy(cur_u[:], pre_u[:]).then_inc(s_cur, 1)

            def gathered(q, c):
                act.wait_ge(s_rf, q * NG + 2 * NG)
                dst = kvT[:, :, c * TT:(c + 1) * TT]
                nc.scalar.copy(dst[:, :, 0:64], ps[:, 0, :].rearrange("p (t h) -> p h t", h=H))
                nc.scalar.copy(dst[:, :, 64:TT], ps[:, 1, 0:(TT - 64) * H].rearrange("p (t h) -> p h t", h=H)).then_inc(s_ke, 1)

            def attend(q, n, c, turned):
                act.wait_ge(s_av, q + 1)
                nc.scalar.copy(vout[:, c, :], ps[0:TT, 6, :]).then_inc(s_avc, 1)
                act.wait_ge(s_aq, q + 1)
                for j in range(2):
                    last = nc.scalar.mul(qt[:, 4 * j:4 * j + 4, :], ps[0:64, 2 + j, 0:4 * TT].rearrange("p (h t) -> p h t", h=4), D ** -0.5)
                last.then_inc(s_aqc, 1)
                J = (c + 1) * TT
                for h in range(H):
                    act.wait_ge(s_nm, q * H + (h + 1))
                    if h >= 2:
                        act.wait_ge(s_tp, q * H + (h - 1))
                    nc.scalar.activation(prob[:, h % 2, 0:J], sm[:, h % 2, 0:J], ACT.Exp, bias=mx[:, 1, h:h + 1],
                                         accum_out=mx[:, 2, h:h + 1]).then_inc(s_e, 1)
                    act.wait_ge(s_tp, q * H + (h + 1))
                    nc.scalar.copy(probT[:, 0:J], ps[0:TT, 6, 0:J]).then_inc(s_tpc, 1)
                act.wait_ge(s_o, q + 2)
                act.wait_ge(s_out, q * 16 + 16)
                nc.scalar.copy(osb[:], ps[0:TT, 7, 0:D]).then_inc(s_osb, 1)

            run(act, pre, front, nothing, nothing, promote, gathered, attend)

        @block.vector
        def _(dve):
            nc.vector.nop().then_inc(s_ke, 1)
            nc.vector.nop().then_inc(s_osb, 1)
            nc.vector.nop().then_inc(s_o, 1)
            nc.vector.nop().then_inc(s_out, 16)

            def pre(b):
                dve.wait_ge(s_pg, b + 1)
                nc.vector.tensor_tensor(mix[:], gate[:], ps[0:64, 3, 0:T], ALU.mult).then_inc(s_chain, 1)
                dve.wait_ge(s_chain, b * 2 + 1)
                nc.vector.tensor_tensor(mix[:], mix[:], ps[0:64, 4, 0:T], ALU.add).then_inc(s_pt, 1)
                dve.wait_ge(s_po, b + 1)
                dve.wait_ge(s_rb, b * 16 + 16)
                if not (isinstance(b, int) and b == 0):
                    dve.wait_ge(s_cur, b)
                nc.vector.scalar_tensor_tensor(pre_h[:], ps[0:64, 5, 0:T], vec[0:64, V_OUTB:V_OUTB + 1], resb[:],
                                               ALU.add, ALU.add).then_inc(s_ph, 1)
                dve.wait_ge(s_ph, b + 1)
                dve.wait_ge(s_pm, b + 1)
                nc.vector.tensor_tensor(cen[:], pre_h[:], ps[0:64, 2, 0:T], ALU.subtract).then_inc(s_pc, 1)
                dve.wait_ge(s_psd, b + 1)
                nc.vector.reciprocal(mix[:], mix[:]).then_inc(s_chain, 1)
                dve.wait_ge(s_pc, b + 1)
                dve.wait_ge(s_chain, b * 2 + 2)
                nc.vector.tensor_tensor(pre_u[:], cen[:], mix[:], ALU.mult).then_inc(s_pu, 1)

            LINKS = 13

            def front(f, b, c):
                count = [0]

                def link(ins):
                    count[0] += 1
                    ins.then_inc(s_fd, 1)
                    dve.wait_ge(s_fd, f * LINKS + count[0])

                def top16(values, best, where, groups):
                    settle(dve)
                    for g in range(groups):
                        last = nc.vector.max(best[:, g, 0:8], values[:, g, :])
                    link(last)
                    settle(dve)
                    for g in range(groups):
                        nc.vector.max_index(where[:, g, 0:8], best[:, g, 0:8], values[:, g, :])
                    for g in range(groups):
                        last = nc.vector.match_replace(values[:, g, :], best[:, g, 0:8], values[:, g, :], LOWEST)
                    link(last)
                    settle(dve)
                    for g in range(groups):
                        last = nc.vector.max(best[:, g, 8:16], values[:, g, :])
                    link(last)
                    settle(dve)
                    for g in range(groups):
                        last = nc.vector.max_index(where[:, g, 8:16], best[:, g, 8:16], values[:, g, :])
                    return last

                dve.wait_ge(s_fsc, f + 1)
                top16(sc, top, topi, 16).then_inc(s_fk, 1)
                dve.wait_ge(s_fk, f + 1)
                link(nc.vector.tensor_copy(topf[:], topi[:]))
                nc.vector.tensor_tensor(topf[:, 0:H, :], topf[:, 0:H, :],
                                        cst["headoff"][0:TT].unsqueeze(2).broadcast_to([TT, H, K]), ALU.add)
                link(nc.vector.tensor_scalar(topf[:, H:, :], topf[:, H:, :], float(NK), None, ALU.mult))
                for src, dst in ((top, cs), (topf, ci)):
                    at = 0
                    for a, na, nb in SEGMENTS:
                        o = dst[:, :, at:at + na * nb]
                        x0, x1 = src[:, 0:H, a:a + na], src[:, H:2 * H, 0:nb]
                        if na > 1 and nb > 1:
                            o = o.rearrange("p h (a b) -> p h a b", b=nb)
                            x0 = x0.unsqueeze(3).broadcast_to([TT, H, na, nb])
                            x1 = x1.unsqueeze(2).broadcast_to([TT, H, na, nb])
                        elif nb > 1:
                            x0 = x0.broadcast_to([TT, H, nb])
                        else:
                            x1 = x1.broadcast_to([TT, H, na])
                        last = nc.vector.tensor_tensor(o, x0, x1, ALU.add)
                        at += na * nb
                link(last)
                link(top16(cs, fin, posi, H))
                nc.vector.tensor_tensor(ew[:], fin[:], fin[:, :, 0:1].broadcast_to([TT, H, K]), ALU.subtract).then_inc(s_few, 1)
                link(nc.vector.tensor_copy(posf[:], posi[:]))
                for h in range(0, H, 2):
                    nc.vector.tensor_tensor(hot[:], posf[:, h:h + 2, :].unsqueeze(3).broadcast_to([TT, 2, K, CAND]),
                                            cst["iota"][0:TT].unsqueeze(1).unsqueeze(1).broadcast_to([TT, 2, K, CAND]),
                                            ALU.is_equal).then_inc(s_hot, 1)
                    dve.wait_ge(s_hot, f * 12 + (3 * (h // 2) + 1))
                    nc.vector.tensor_tensor(hot[:], hot[:], ci[:, h:h + 2, :].unsqueeze(2).broadcast_to([TT, 2, K, CAND]),
                                            ALU.mult).then_inc(s_hot, 1)
                    dve.wait_ge(s_hot, f * 12 + (3 * (h // 2) + 2))
                    nc.vector.tensor_reduce(idxf[:, h:h + 2, :], hot[:], AX_X, ALU.add).then_inc(s_hot, 1)
                    dve.wait_ge(s_hot, f * 12 + (3 * (h // 2) + 3))
                dve.wait_ge(s_fexp, f + 1)
                link(nc.vector.tensor_reduce(esum[:], ew[:], AX_X, ALU.add))
                link(nc.vector.reciprocal(esum[:], esum[:]))
                nc.vector.tensor_tensor(ew[:], ew[:], esum[:].unsqueeze(2).broadcast_to([TT, H, K]), ALU.mult).then_inc(s_fi, 1)
                assert count[0] == LINKS

            def turn(f, c):
                dve.wait_ge(s_ft, f + 1)
                if not (isinstance(f, int) and f < NT):
                    dve.wait_ge(s_rf, f * NG - (NT - 2) * NG)
                nc.vector.tensor_copy(idxT[:, c, :], ps[:, 2, 0:TT])
                nc.vector.tensor_copy(wT[:, c, :], ps[:, 2, 128:128 + TT]).then_inc(s_fT, 1)

            def weigh(q, c):
                dve.wait_ge(s_rf, q * NG + NG)
                dve.wait_ge(s_fT, q + 1)
                nc.vector.tensor_tensor(wmat[:], wT[:, c, :].unsqueeze(2).broadcast_to([128, TT, H]),
                                        cst["mask8"].unsqueeze(1).broadcast_to([128, TT, H]), ALU.mult).then_inc(s_wm, 1)

            def attend(q, n, c, turned):
                J = (c + 1) * TT
                mask = cst["causal"][0:TT, T - c * TT:T + TT]

                def scaled_identity(h):
                    dve.wait_ge(s_e, q * H + (h + 1))
                    nc.vector.reciprocal(mx[:, 3, h:h + 1], mx[:, 2, h:h + 1]).then_inc(s_ri, 1)
                    dve.wait_ge(s_ri, q * H + (h + 1))
                    if h >= 2:
                        dve.wait_ge(s_tp, q * H + (h - 1))
                    nc.vector.tensor_scalar(dg[:, h % 2, :], ident[0:TT, 0:TT], mx[:, 3, h:h + 1], None,
                                            ALU.mult).then_inc(s_dg, 1)

                for h in range(H):
                    dve.wait_ge(s_s, q * H + (h + 1))
                    if h >= 2:
                        dve.wait_ge(s_e, q * H + (h - 1))
                    settle(dve)
                    nc.vector.tensor_tensor_reduce(sm[:, h % 2, 0:J], ps[0:TT, 4 + h % 2, 0:J], mask, 1.0, LOWEST,
                                                   ALU.add, ALU.max, mx[:, 0, h:h + 1]).then_inc(s_sm, 1)
                    dve.wait_ge(s_sm, q * H + (h + 1))
                    nc.vector.tensor_scalar(mx[:, 1, h:h + 1], mx[:, 0, h:h + 1], -1.0, None, ALU.mult).then_inc(s_nm, 1)
                    if h >= 1:
                        scaled_identity(h - 1)
                scaled_identity(H - 1)

            run(dve, pre, front, turn, weigh, nothing, nothing, attend)


def kernel(**inputs):
    from concourse.bacc import Bacc
    from concourse.bass_utils import run_bass_kernel_spmd

    pack, early = pack_constants(inputs)
    table = np.concatenate([inputs["L0_ffn_keys_table"], inputs["L0_ffn_values_table"]], axis=1)
    arrays = {"x_dram": np.ascontiguousarray(inputs["x"]), "pack_dram": pack, "early_dram": early,
              "table_dram": np.ascontiguousarray(table)}
    nc = Bacc("TRN2", target_bir_lowering=False, num_devices=1)
    args = [nc.dram_tensor(name, a.shape, mybir.dt.from_np(a.dtype), kind="ExternalInput").ap()
            for name, a in arrays.items()]
    result = nc.dram_tensor("out_dram", (B, T, D), F32, kind="ExternalOutput").ap()
    build(nc, *args, result)
    r = run_bass_kernel_spmd(nc, [arrays], core_ids=[0])
    return r.results[0]["out_dram"]


def pack_constants(inputs):
    w = {k[3:]: np.asarray(v) for k, v in inputs.items() if k != "x"}

    def two(a, b):
        z = np.zeros((128, 128), np.float32)
        z[0:64, 0:64], z[64:, 64:] = a, b
        return z

    def low(a):
        z = np.zeros((128, a.shape[1]), np.float32)
        z[0:a.shape[0]] = a
        return z

    def both(v):
        return np.concatenate([v, v])[:, None]

    f = {"ident": np.eye(128, dtype=np.float32)}
    f["mean"] = two(np.full((64, 64), 1 / 64, np.float32), np.full((64, 64), 1 / 64, np.float32))
    f["win0"] = two(w["tok_W_in"][0], w["tok_W_in"][0])
    f["win1"] = two(w["tok_W_in"][1], w["tok_W_in"][1])
    f["wout1"] = two(w["tok_W_out"][1], w["tok_W_out"][1])
    f["wout0"] = two(w["tok_W_out"][0], w["tok_W_out"][0])
    vec = [both(w["tok_b_in"][0]), both(w["tok_b_in"][1]), both(w["tok_b_out"][1]), both(w["tok_b_out"][0]),
           both(w["tok_core_diag"]), both(w["attn_ln_g"]), both(w["attn_ln_b"]),
           np.broadcast_to(w["tok_conv_filter"], (128, TAPS))]
    vec += [low(w["attn_gate_b"][:, None]), low(w["attn_out_b"][:, None]),
            np.full((128, 1), EPS, np.float32)]
    f["vecs"] = np.concatenate(vec, axis=1)
    dirs = np.zeros((128, 2 * B), np.float32)
    for i in (0, 32, 64):
        dirs[i, 0:B] = dirs[i + 1, B:] = 1.0
    f["dirsel"] = dirs
    for side in ("ih", "hh"):
        f["w" + side] = np.concatenate([w[f"attn_fwd_w_{side}"].T, w[f"attn_rev_w_{side}"].T])
        rows = np.zeros((128, 192), np.float32)
        for i in (0, 32, 64):
            rows[i], rows[i + 1] = w[f"attn_fwd_b_{side}"], w[f"attn_rev_b_{side}"]
        f["b" + side] = rows
    f["gatew"] = w["attn_gate_w"].T
    eye = np.eye(64, dtype=np.float32)
    f["diff"] = np.concatenate([eye, -eye])
    f["pickrev"] = np.concatenate([0 * eye, eye])
    f["outw"] = low(w["attn_out_w"].T)
    f["mask8"] = np.repeat(np.eye(H, dtype=np.float32), K, axis=0)
    f["iota"] = np.broadcast_to(np.arange(CAND, dtype=np.float32), (128, CAND))
    tri = np.where(np.arange(128)[:, None] >= np.arange(TT)[None], 0.0, LOWEST).astype(np.float32)
    f["causal"] = np.concatenate([np.zeros((128, T), np.float32), tri], axis=1)
    f["headoff"] = np.broadcast_to(np.arange(H, dtype=np.float32) * NK * NK, (128, H))
    qpk = w["ffn_Wq_pk"].T.reshape(4, 128, 64)
    f["wqpkT"] = np.concatenate(list(qpk), axis=1)
    keys = np.zeros((2, 2, 4, 32, 4, 64), np.float32)
    for h in range(4):
        keys[:, :, h, :, h, :] = w["ffn_pk_keys"].reshape(2, 64, 2, 4, 32)[:, :, :, h].transpose(0, 2, 3, 1)
    f["keys"] = np.concatenate(list(keys.reshape(4, 128, 256)), axis=1)
    f["wq"] = low(w["ffn_Wq"])
    wo = np.zeros((128, 512), np.float32)
    wo[64:] = w["ffn_Wo"].reshape(8, 64, 64).transpose(1, 0, 2).reshape(64, 512)
    f["wo"] = wo
    for name, width in FIELDS + EARLY:
        assert f[name].shape == (128, width), (name, f[name].shape)
    return [np.ascontiguousarray(np.concatenate([f[name] for name, _ in names], axis=1)) for names in (FIELDS, EARLY)]
```
